# Optimizing a Trainium2 kernel written in Bass

```python
import numpy as np
import jax
import jax.numpy as jnp

def _softmax(x, axis=-1):
    return jax.nn.softmax(x, axis=axis)

def _gelu(x):
    return jax.nn.gelu(x, approximate=True)

def _silu(x):
    return jax.nn.silu(x)

def _sigmoid(x):
    return jax.nn.sigmoid(x)

def _layernorm(x, axis=-1, eps=1e-05):
    m = jnp.mean(x, axis=axis, keepdims=True)
    v = jnp.var(x, axis=axis, keepdims=True)
    return (x - m) / jnp.sqrt(v + eps)

def _scatter_add(tgt, idx, src, axis=0):
    return tgt.at[idx].add(src)

def _segment_sum(src, seg, n):
    return jax.ops.segment_sum(src, seg, n)
kernel_name = 'mk_vit_tower_d1_tok_img512_r4_f4bdf6'

def setup_inputs(seed: int=0):
    np.random.seed(seed)
    _w = jnp.asarray

    def _rec_inputs():
        import jax
        import jax.numpy as jnp
        _rk = jax.random.key(seed)
        x = -0.000121822 + 0.999869 * jax.random.normal(jax.random.fold_in(_rk, 1), (128, 3, 196, 196), jnp.float32)
        return x
    x = _rec_inputs()

    def _L0_tok_setup():
        import jax, jax.numpy as jnp
        import numpy as np
        B, C, H, N_P, HID = (64, 3, 196, 14, 128)
        P = H // N_P
        IN_DIM = C * P * P
        SEQ = N_P * N_P + 1

        def sinusoidal_position(length, d):
            pos = jnp.arange(length, dtype=jnp.float32)[:, None]
            i = jnp.arange(d)[None, :]
            angle = pos / jnp.power(10000.0, (2 * (i // 2)).astype(jnp.float32) / d)
            return jnp.where(i % 2 == 0, jnp.sin(angle), jnp.cos(angle)).astype(jnp.float32)
        key = jax.random.key(seed)
        k_img, k_w, k_b, k_tok = jax.random.split(key, 4)
        img = jax.random.normal(k_img, (B, C, H, H), dtype=jnp.float32)
        W = jax.random.normal(k_w, (HID, IN_DIM), dtype=jnp.float32) / np.sqrt(IN_DIM)
        b = jax.random.normal(k_b, (HID,), dtype=jnp.float32) * 0.01
        token = jax.random.uniform(k_tok, (1, HID), dtype=jnp.float32)
        pos = sinusoidal_position(SEQ, HID)
        return {'img': img, 'W': W, 'b': b, 'token': token, 'pos': pos}
    _L0_tok_all = _L0_tok_setup()
    _L0_tok_in = {k: v for k, v in _L0_tok_all.items() if k in ('W', 'b', 'token', 'pos')}
    del _L0_tok_all

    def _L0_attn_setup():
        import jax, jax.numpy as jnp
        import numpy as np
        import math
        BATCH, LEN, HID, STATE = (16, 1024, 128, 128)
        DT_MIN, DT_MAX = (0.001, 0.1)
        STEP_RESCALE = 1.0
        CONJ_SYM = True

        def _s5_forward(inputs, lambda_real, lambda_imag, B, C, D, log_step):
            lam = (lambda_real + 1j * lambda_imag).astype(jnp.complex64)
            step = STEP_RESCALE * jnp.exp(log_step[:, 0])
            lambda_bar = jnp.exp(lam * step.astype(jnp.complex64))
            B_c = (B[..., 0] + 1j * B[..., 1]).astype(jnp.complex64)
            C_c = (C[..., 0] + 1j * C[..., 1]).astype(jnp.complex64)
            b_bar = ((lambda_bar - 1.0) / lam)[:, None] * B_c
            bu = jnp.einsum('blh,ph->lbp', inputs.astype(jnp.complex64), b_bar)
            L = inputs.shape[1]
            a = jnp.broadcast_to(lambda_bar[None, None, :], (L, 1, STATE))

            def combine(e1, e2):
                a1, b1 = e1
                a2, b2 = e2
                return (a2 * a1, a2 * b1 + b2)
            _, states = jax.lax.associative_scan(combine, (a, bu))
            y = jnp.einsum('lbp,hp->blh', states, C_c)
            out = 2.0 * y.real if CONJ_SYM else y.real
            return out + D * inputs
        key = jax.random.key(seed)
        ks = jax.random.split(key, 7)
        inputs = jax.random.normal(ks[0], (BATCH, LEN, HID), jnp.float32)
        lambda_real = -0.5 * jnp.abs(jax.random.normal(ks[1], (STATE,), jnp.float32)) - 0.001
        lambda_imag = jnp.pi * jax.random.normal(ks[2], (STATE,), jnp.float32)
        B = jax.random.normal(ks[3], (STATE, HID, 2), jnp.float32) * (1.0 / math.sqrt(HID))
        C = jax.random.normal(ks[4], (HID, STATE, 2), jnp.float32) * (1.0 / math.sqrt(STATE))
        D = jax.random.normal(ks[5], (HID,), jnp.float32)
        u = jax.random.uniform(ks[6], (STATE, 1), jnp.float32)
        log_step = u * (math.log(DT_MAX) - math.log(DT_MIN)) + math.log(DT_MIN)
        return dict(inputs=inputs, lambda_real=lambda_real, lambda_imag=lambda_imag, B=B, C=C, D=D, log_step=log_step)
    _L0_attn_all = _L0_attn_setup()
    _L0_attn_in = {k: v for k, v in _L0_attn_all.items() if k in ('lambda_real', 'lambda_imag', 'B', 'C', 'D', 'log_step')}
    del _L0_attn_all

    def _L0_ffn_setup():
        import jax, jax.numpy as jnp
        import numpy as np
        EPS = 1e-09
        LN_EPS = 1e-05

        def _layernorm(x, gamma):
            x = x.astype(jnp.float32)
            mu = jnp.mean(x, axis=-1, keepdims=True)
            var = jnp.var(x, axis=-1, keepdims=True)
            return (x - mu) * jax.lax.rsqrt(var + LN_EPS) * gamma
        key = jax.random.key(seed)
        ks = jax.random.split(key, 5)
        b, n, d, e, h = (4, 256, 128, 6, 512)
        x = jax.random.normal(ks[0], (b, n, d), dtype=jnp.float32)
        w_gating = jax.random.normal(ks[1], (d, e), dtype=jnp.float32)
        std1 = 1.0 / np.sqrt(h)
        std2 = 1.0 / np.sqrt(d)
        w1 = jax.random.uniform(ks[2], (e, d, h), jnp.float32, -std1, std1)
        w2 = jax.random.uniform(ks[3], (e, h, d), jnp.float32, -std2, std2)
        gamma = jnp.ones((d,), dtype=jnp.float32)
        return {'x': x, 'w_gating': w_gating, 'gamma': gamma, 'w1': w1, 'w2': w2}
    _L0_ffn_all = _L0_ffn_setup()
    _L0_ffn_in = {k: v for k, v in _L0_ffn_all.items() if k in ('w_gating', 'gamma', 'w1', 'w2')}
    del _L0_ffn_all
    return {'x': x, 'L0_tok_W': _L0_tok_in['W'], 'L0_tok_b': _L0_tok_in['b'], 'L0_tok_token': _L0_tok_in['token'], 'L0_tok_pos': _L0_tok_in['pos'], 'L0_attn_lambda_real': _L0_attn_in['lambda_real'], 'L0_attn_lambda_imag': _L0_attn_in['lambda_imag'], 'L0_attn_B': _L0_attn_in['B'], 'L0_attn_C': _L0_attn_in['C'], 'L0_attn_D': _L0_attn_in['D'], 'L0_attn_log_step': _L0_attn_in['log_step'], 'L0_ffn_w_gating': _L0_ffn_in['w_gating'], 'L0_ffn_gamma': _L0_ffn_in['gamma'], 'L0_ffn_w1': _L0_ffn_in['w1'], 'L0_ffn_w2': _L0_ffn_in['w2']}

def reference(x, L0_tok_W, L0_tok_b, L0_tok_token, L0_tok_pos, L0_attn_lambda_real, L0_attn_lambda_imag, L0_attn_B, L0_attn_C, L0_attn_D, L0_attn_log_step, L0_ffn_w_gating, L0_ffn_gamma, L0_ffn_w1, L0_ffn_w2):
    import jax
    import jax.numpy as jnp

    def _L0_tok_ref(img, W, b, token, pos):
        import jax, jax.numpy as jnp
        import numpy as np
        B, C, H, N_P, HID = (64, 3, 196, 14, 128)
        P = H // N_P
        IN_DIM = C * P * P
        SEQ = N_P * N_P + 1

        def sinusoidal_position(length, d):
            pos = jnp.arange(length, dtype=jnp.float32)[:, None]
            i = jnp.arange(d)[None, :]
            angle = pos / jnp.power(10000.0, (2 * (i // 2)).astype(jnp.float32) / d)
            return jnp.where(i % 2 == 0, jnp.sin(angle), jnp.cos(angle)).astype(jnp.float32)
        Bn = img.shape[0]
        patches = img.reshape(Bn, C, N_P, P, N_P, P)
        patches = patches.transpose(0, 2, 4, 1, 3, 5).reshape(Bn, N_P * N_P, IN_DIM)
        tokens = jnp.einsum('bsd,hd->bsh', patches, W) + b
        cls = jnp.broadcast_to(token[None, :, :], (Bn, 1, HID))
        out = jnp.concatenate([cls, tokens], axis=1) + pos
        return out

    def _L0_attn_ref(inputs, lambda_real, lambda_imag, B, C, D, log_step):
        import jax, jax.numpy as jnp
        import numpy as np
        import math
        BATCH, LEN, HID, STATE = (16, 1024, 128, 128)
        DT_MIN, DT_MAX = (0.001, 0.1)
        STEP_RESCALE = 1.0
        CONJ_SYM = True

        def _s5_forward(inputs, lambda_real, lambda_imag, B, C, D, log_step):
            lam = (lambda_real + 1j * lambda_imag).astype(jnp.complex64)
            step = STEP_RESCALE * jnp.exp(log_step[:, 0])
            lambda_bar = jnp.exp(lam * step.astype(jnp.complex64))
            B_c = (B[..., 0] + 1j * B[..., 1]).astype(jnp.complex64)
            C_c = (C[..., 0] + 1j * C[..., 1]).astype(jnp.complex64)
            b_bar = ((lambda_bar - 1.0) / lam)[:, None] * B_c
            bu = jnp.einsum('blh,ph->lbp', inputs.astype(jnp.complex64), b_bar)
            L = inputs.shape[1]
            a = jnp.broadcast_to(lambda_bar[None, None, :], (L, 1, STATE))

            def combine(e1, e2):
                a1, b1 = e1
                a2, b2 = e2
                return (a2 * a1, a2 * b1 + b2)
            _, states = jax.lax.associative_scan(combine, (a, bu))
            y = jnp.einsum('lbp,hp->blh', states, C_c)
            out = 2.0 * y.real if CONJ_SYM else y.real
            return out + D * inputs
        return _s5_forward(inputs, lambda_real, lambda_imag, B, C, D, log_step)

    def _L0_ffn_ref(x, w_gating, gamma, w1, w2):
        import jax, jax.numpy as jnp
        import numpy as np
        EPS = 1e-09
        LN_EPS = 1e-05

        def _layernorm(x, gamma):
            x = x.astype(jnp.float32)
            mu = jnp.mean(x, axis=-1, keepdims=True)
            var = jnp.var(x, axis=-1, keepdims=True)
            return (x - mu) * jax.lax.rsqrt(var + LN_EPS) * gamma
        b, n, d = x.shape
        E = w_gating.shape[-1]
        C = max(min(n, int(n * 6.0 / E)), 4)
        raw = jnp.einsum('bnd,de->bne', x, w_gating)
        probs = jax.nn.softmax(raw, axis=-1)
        gate1 = jnp.max(probs, axis=-1)
        idx1 = jnp.argmax(probs, axis=-1)
        mask1 = jax.nn.one_hot(idx1, E, dtype=jnp.float32)
        gates_wo1 = probs * (1.0 - mask1)
        gate2 = jnp.max(gates_wo1, axis=-1)
        denom = gate1 + gate2 + EPS
        gate1 = gate1 / denom
        pos1 = (jnp.cumsum(mask1, axis=-2) - mask1) * mask1
        mask1 = mask1 * (pos1 < float(C)).astype(jnp.float32)
        mask1_flat = jnp.sum(mask1, axis=-1)
        pos1_flat = jnp.sum(pos1, axis=-1).astype(jnp.int32)
        gate1 = gate1 * mask1_flat
        combine = gate1[..., None, None] * mask1_flat[..., None, None] * jax.nn.one_hot(idx1, E, dtype=jnp.float32)[..., None] * jax.nn.one_hot(pos1_flat, C, dtype=jnp.float32)[..., None, :]
        dispatch = (combine != 0).astype(jnp.float32)
        expert_in = jnp.einsum('bnd,bnec->ebcd', x, dispatch)
        xn = _layernorm(expert_in, gamma)
        hidden = jax.nn.gelu(jnp.einsum('ebcd,edh->ebch', xn, w1), approximate=False)
        expert_out = jnp.einsum('ebch,ehd->ebcd', hidden, w2)
        out = jnp.einsum('ebcd,bnec->bnd', expert_out, combine)
        return out
    h = _L0_tok_ref(x, L0_tok_W, L0_tok_b, L0_tok_token, L0_tok_pos)
    h = h + _L0_attn_ref(_layernorm(h, axis=-1), L0_attn_lambda_real, L0_attn_lambda_imag, L0_attn_B, L0_attn_C, L0_attn_D, L0_attn_log_step)
    h = h + _L0_ffn_ref(_layernorm(h, axis=-1), L0_ffn_w_gating, L0_ffn_gamma, L0_ffn_w1, L0_ffn_w2)
    return h

_drawn_inputs = setup_inputs


def setup_inputs(seed=0):
    import zlib

    import numpy as np

    out = dict(_drawn_inputs(seed))
    spreads = {'L0_ffn_gamma': (1.0, 0.6)}
    factors = {'L0_tok_b': 4.578}
    for name, (base, spread) in spreads.items():
        noise = np.random.default_rng([zlib.crc32(name.encode()), seed]).standard_normal(out[name].shape)
        drawn = base * np.exp(spread * noise) if base else spread * noise
        out[name] = jnp.asarray(drawn.astype(out[name].dtype))
    for name, factor in factors.items():
        out[name] = (out[name] * factor).astype(out[name].dtype)
    return out
```

```python
from contextlib import ExitStack

import concourse.bass as bass
from concourse import mybir

ALU = mybir.AluOpType
ACT = mybir.ActivationFunctionType
AX = mybir.AxisListType.X
F32 = mybir.dt.float32
BF16 = mybir.dt.bfloat16
I32 = mybir.dt.int32
U32 = mybir.dt.uint32

B = 128
HID = 128
GRID = 14
IN_DIM = 3 * 14 * 14
SEQ = GRID * GRID + 1
KC = IN_DIM // 128
KT = IN_DIM - KC * 128
TQ = 4
NQ = (SEQ - 1) // TQ
U = 7
E = 6
FF = 512
FC = FF // 128
EPS = 1e-5
GATE_EPS = 1e-9
CAPACITY = max(min(SEQ, int(SEQ * 6.0 / E)), 4)
assert CAPACITY == SEQ and NQ % U == 0

NTOK = B * SEQ
TILE = 512
TJ = TILE // 128
REGION = NTOK + TILE
NT = (NTOK + E * (TILE - 1)) // TILE
NT += NT % 2
LISTED = 132
RAW = HID
ROW = HID + E
NOWHERE = float(NTOK + 1000)
MAXT = (NTOK + TILE - 1) // TILE

V_LR, V_LI, V_STEP, V_D, V_B, V_TOK, V_GAMMA, V_IMG = range(8)
C_ID, C_TRI, C_WT = 0, 128, 256
C_BASE = C_WT + TQ * E
C_GRID = C_BASE + E
C_K = C_GRID + MAXT
C_END = C_K + NT


def build(nc, x_main, x_tail, w_main, w_tail, vecs, posT, b_ri, c_hp, c_ph, wg, w1, w2, consts, out):
    with ExitStack() as ctx:
        def sb(name, shape, dt=F32):
            return ctx.enter_context(nc.sbuf_tensor(name, shape, dt))

        def sem(name):
            return ctx.enter_context(nc.semaphore(name))

        bank = [ctx.enter_context(nc.psum_tensor(f"bank{n}", [128, 512], F32)) for n in range(8)]
        ps_h, ps_ht, ps_ut, ps_bur, ps_bui, ps_o0, ps_o1, ps_rank = bank
        ps_o = [ps_o0, ps_o1]
        ps_xt, ps_g, ps_y = bank[0], bank[1:5], bank[5:7]

        lists = nc.dram_tensor("lists", [E * REGION + TILE, LISTED], F32).ap()
        w1_scaled = nc.dram_tensor("w1_scaled", [E * HID, FF], F32).ap()

        cst = sb("cst", [128, C_END])
        ident = cst[:, C_ID:C_ID + 128]
        tie_weight = cst[:, C_WT:C_WT + TQ * E].rearrange("p (t e) -> p t e", e=E)
        vec = sb("vec", [128, 8])
        pos = sb("pos", [128, SEQ])
        wm = sb("wm", [128, KC, HID])
        wt = sb("wt", [KT, HID])
        bri = sb("bri", [128, 2, HID])
        chp = sb("chp", [128, 2, HID])
        wg_sb = sb("wg_sb", [128, E])
        lam = sb("lam", [128, 24])
        bbar = sb("bbar", [128, 2, HID])
        bt = sb("bt", [128, 2, HID])
        rhs_v = sb("rhs_v", [128, ROW])
        rhs_s = sb("rhs_s", [128, 2, ROW])
        tri = sb("tri", [128, 128], BF16)
        ones = sb("ones", [128, 128], BF16)
        ones_mean = sb("ones_mean", [128, 128])
        zeros = sb("zeros", [128, 128])
        eps_t = sb("eps_t", [128, TQ])
        half_t = sb("half_t", [128, 2, TQ])
        neg_t = sb("neg_t", [128, TQ])
        four_t = sb("four_t", [128, TQ])
        xm = sb("xm", [128, U, KC, TQ * B])
        xt = sb("xt", [KT, U, TQ * B])
        h_t = sb("h_t", [128, 3, TQ, B])
        u_b = sb("u_b", [128, TQ, HID])
        u_t = sb("u_t", [128, TQ, B])
        v_t = sb("v_t", [128, 3, TQ, B])
        states = sb("states", [128, TQ, 2, B])
        decayed = sb("decayed", [128, 2, 2, B])
        st1 = sb("st1", [128, TQ, 6])
        mv1 = sb("mv1", [128, TQ, 2])
        ve1 = sb("ve1", [128, TQ])
        rs1 = sb("rs1", [128, TQ])
        nm1 = sb("nm1", [128, TQ])
        nmr1 = sb("nmr1", [128, TQ])
        rows = sb("rows", [128, U, TQ, ROW])
        st2 = sb("st2", [128, TQ, 6])
        mv2 = sb("mv2", [128, TQ, 2])
        ve2 = sb("ve2", [128, 2, TQ])
        rs2 = sb("rs2", [128, 2, TQ])
        nm2 = sb("nm2", [128, TQ])
        out_row = sb("out_row", [128, TQ])
        top = sb("top", [128, TQ])
        below = sb("below", [128, TQ, E])
        key = sb("key", [128, TQ, E])
        key_top = sb("key_top", [128, TQ])
        chosen = sb("chosen", [128, TQ, E], BF16)
        scaled = sb("scaled", [128, TQ, E])
        expd = sb("expd", [128, TQ, E])
        exp_sum = sb("exp_sum", [128, TQ])
        others = sb("others", [128, TQ, E])
        second = sb("second", [128, TQ])
        gate_den = sb("gate_den", [128, TQ])
        gate_den1 = sb("gate_den1", [128, TQ])
        place = sb("place", [128, TQ, E])
        listed_at = sb("listed_at", [128, TQ, E])
        dest_f = sb("dest_f", [128, TQ])
        dest = sb("dest", [128, U, TQ], U32)
        base = sb("base", [128, 2, E])
        filler = sb("filler", [128, TJ, LISTED])
        count = sb("count", [1, E])
        cmp_t = sb("cmp_t", [1, E, MAXT])
        ntile = sb("ntile", [1, E])
        one_e = sb("one_e", [1, E])
        cum = sb("cum", [1, E])
        passed = sb("passed", [1, NT, E])
        expert_f = sb("expert_f", [1, NT])
        before = sb("before", [1, NT, E])
        before_f = sb("before_f", [1, NT])
        start_f = sb("start_f", [1, 3, NT])
        start_i = sb("start_i", [1, NT], I32)
        expert_i = sb("expert_i", [1, NT], I32)
        base_i = sb("base_i", [1, E], I32)
        lt = sb("lt", [128, 2, TJ, LISTED])
        w1_t = sb("w1_t", [128, 2, FC, 128])
        w2_t = sb("w2_t", [128, 2, FC, HID])
        xn = sb("xn", [128, TJ, HID])
        xn_t = sb("xn_t", [128, TILE])
        hidden = sb("hidden", [128, 2, FC, TILE])
        res = sb("res", [128, 2, TJ, HID])
        place_i = sb("place_i", [128, 2, TJ], U32)
        w1_in = xm[:, 0:2, :, :].rearrange("p u c n -> p (u c n)")[:, 0:E * FF].rearrange("p (e f) -> p e f", e=E)
        w1_out = xm[:, 2:4, :, :].rearrange("p u c n -> p (u c n)")[:, 0:E * FF].rearrange("p (e f) -> p e f", e=E)

        consts_landed, vec_landed, w_landed = sem("consts_landed"), sem("vec_landed"), sem("w_landed")
        bc_landed = sem("bc_landed")
        pool_passed = sem("pool_passed")
        memsets_done, setup_dve, setup_act, setup_pe, setup_chain = (
            sem("memsets_done"), sem("setup_dve"), sem("setup_act"), sem("setup_pe"), sem("setup_chain"))
        x_landed = [sem(f"x_landed{q}") for q in range(U)]
        h_summed, h_copied = sem("h_summed"), sem("h_copied")
        hb_ready, moments1, stats1_parts = sem("hb_ready"), sem("moments1"), sem("stats1_parts")
        ve1_ready, nm1_ready, rs1_ready, norm1 = sem("ve1_ready"), sem("nm1_ready"), sem("rs1_ready"), sem("norm1")
        u_ready, ut_ready, ut_copied, v_ready = sem("u_ready"), sem("ut_ready"), sem("ut_copied"), sem("v_ready")
        bu_ready = sem("bu_ready")
        decay_done, state_done = sem("decay_done"), sem("state_done")
        out_ready, row_copied = sem("out_ready"), sem("row_copied")
        stats2_parts, moments2 = sem("stats2_parts"), sem("moments2")
        ve2a_ready, ve2b_ready, ve2c_ready = sem("ve2a_ready"), sem("ve2b_ready"), sem("ve2c_ready")
        rs2_ready, nm2_ready, nmr2_ready = sem("rs2_ready"), sem("nm2_ready"), sem("nmr2_ready")
        outrow_ready, meta_ready = sem("outrow_ready"), sem("meta_ready")
        top_ready, below_ready, key_ready, keytop_ready, chosen_ready = (
            sem("top_ready"), sem("below_ready"), sem("key_ready"), sem("keytop_ready"), sem("chosen_ready"))
        scaled_ready, exp_ready, sum_ready, others_ready, second_ready = (
            sem("scaled_ready"), sem("exp_ready"), sem("sum_ready"), sem("others_ready"), sem("second_ready"))
        den_ready, den1_ready, gate_ready = sem("den_ready"), sem("den1_ready"), sem("gate_ready")
        rank_ready, place_ready, base_ready, at_ready, destf_ready, dest_ready = (
            sem("rank_ready"), sem("place_ready"), sem("base_ready"), sem("at_ready"), sem("destf_ready"),
            sem("dest_ready"))
        listed = [sem(f"listed{q}") for q in range(U)]
        rows_left = sem("rows_left")
        plan_step, plan_ready, filled, w1_loaded, w1_scaled_ready, w1_stored = (
            sem("plan_step"), sem("plan_ready"), sem("filled"), sem("w1_loaded"), sem("w1_scaled_ready"),
            sem("w1_stored"))
        tile_landed = [sem(f"tile_landed{p}") for p in range(2)]
        xn_ready, xt_ready, xt_copied = sem("xn_ready"), sem("xt_ready"), sem("xt_copied")
        up_ready, gelu_done = sem("up_ready"), sem("gelu_done")
        y_ready, combined, placei_ready = sem("y_ready"), sem("combined"), sem("placei_ready")
        stored = [sem(f"stored{p}") for p in range(2)]

        block = ctx.enter_context(nc.Block())

        def wait(eng, s, value):
            if not (isinstance(value, int) and value <= 0):
                eng.wait_ge(s, value)

        def exists(m):
            return not isinstance(m, int) or 0 <= m <= NQ

        def steps_of(m):
            return 1 if isinstance(m, int) and m == 0 else TQ

        def last_t(m):
            return TQ * m + 1

        HSLOT = [0, 1, 0, 1, 0, 1, 2]

        def for_steps(eng, step):
            for q in range(U):
                step(q + 1, q)
            with eng.Fori(1, NQ // U) as i:
                first = i * U
                for q in range(U):
                    step(first + (q + 1), q)
            for m in range(NQ + 1, NQ + 6):
                step(m, (m - 1) % U)

        def slot(q, lag):
            return (q - lag) % U

        @block.sync
        def _(sp):
            def load(m, q):
                wait(sp, h_summed, m - U)
                ix = m - 1
                sp.dma_start(xm[:, q, :, :], x_main[ix] if isinstance(m, int) else
                             x_main[bass.ds(ix, 1)].rearrange("o p c n -> (o p) c n")).then_inc(x_landed[q], 16)
                sp.dma_start(xt[:, q, :], x_tail[ix] if isinstance(m, int) else
                             x_tail[bass.ds(ix, 1)].rearrange("o p n -> (o p) n")).then_inc(x_landed[q], 16)

            sp.dma_start(cst[:], consts).then_inc(consts_landed, 16)
            for q in range(U):
                load(q + 1, q)
            with sp.Fori(1, NQ // U) as i:
                first = sp.snap(i * U)
                for q in range(U):
                    load(first + (q + 1), q)

            sp.wait_ge(h_summed, NQ)
            sp.dma_start(w1_in, w1.rearrange("e d f -> d e f")).then_inc(w1_loaded, 16)
            sp.wait_ge(w1_scaled_ready, 1)
            sp.dma_start(w1_scaled.rearrange("(e d) f -> d e f", e=E), w1_out).then_inc(w1_stored, 16)

            sp.wait_ge(plan_ready, 1)
            for e in range(E):
                end = sp.value_load(base_i[0:1, e:e + 1], min_val=e * REGION, max_val=e * REGION + NTOK)
                sp.dma_start(lists[bass.ds(end, TILE), :].rearrange("(j p) c -> p j c", p=128), filler[:])\
                    .then_inc(filled, 16)
            sp.dma_start(lists[E * REGION:E * REGION + TILE, :].rearrange("(j p) c -> p j c", p=128), filler[:])\
                .then_inc(filled, 16)
            sp.wait_ge(filled, 16 * (E + 1))
            sp.wait_ge(w1_stored, 16)
            for q in range(U):
                sp.wait_ge(listed[q], 16 * TQ * (NQ // U) + (16 if q == U - 1 else 0))

            def load_tile(k, p):
                wait(sp, combined, k - 1)
                at = slice(k, k + 1) if isinstance(k, int) else bass.ds(k, 1)
                row = sp.value_load(start_i[0:1, at], min_val=0, max_val=E * REGION)
                sp.dma_start(lt[:, p, :, :], lists[bass.ds(row, TILE), :].rearrange("(j p) c -> p j c", p=128))\
                    .then_inc(tile_landed[p], 16)
                ex = sp.value_load(expert_i[0:1, at], min_val=0, max_val=E - 1)
                sp.dma_start(w1_t[:, p, :, :].rearrange("p c f -> p (c f)"), w1_scaled[bass.ds(ex * HID, HID), :])\
                    .then_inc(tile_landed[p], 16)
                sp.dma_start(w2_t[:, p, :, :].rearrange("p c d -> p (c d)"),
                             w2[bass.ds(ex, 1)].rearrange("o (p c) d -> (o p) (c d)", c=FC))\
                    .then_inc(tile_landed[p], 16)

            for p in range(2):
                load_tile(p, p)
            with sp.Fori(1, NT // 2) as i:
                for p in range(2):
                    load_tile(i * 2 + p, p)
            for p in range(2):
                sp.wait_ge(stored[p], 16 * TJ * (NT // 2))

        @block.tensor
        def _(pe):
            pe.wait_ge(w_landed, 16 * 5)
            pe.wait_ge(memsets_done, 1)
            pe.matmul(ps_h[:, 0:E], ones_mean[:], wg_sb[:], start=True, stop=True).then_inc(setup_pe, 1)
            pe.wait_ge(consts_landed, 16)
            pe.wait_ge(setup_dve, 1)
            for c in range(2):
                last = pe.transpose(ps_ht[:, c * 128:(c + 1) * 128], bbar[:, c, :], ident)
            last.then_inc(setup_pe, 1)
            for c in range(2):
                last = pe.matmul(ps_ut[:, c * 64:c * 64 + E], chp[:, c, :], rhs_v[:, HID:ROW], start=True, stop=True)
            last.then_inc(setup_pe, 1)

            def step(m, q):
                a, b = m - 1, m - 2
                if exists(a):
                    pe.wait_ge(h_copied, m)
                    wait(pe, u_ready, m - 1)
                    if isinstance(m, int) and m == 1:
                        pe.wait_ge(setup_dve, 2)
                    for t in range(steps_of(a)):
                        last = pe.transpose(ps_ht[:, t * 128:(t + 1) * 128], h_t[:, HSLOT[slot(q, 1)], t, :], ident)
                    last.then_inc(hb_ready, 1)
                d = m - 4
                if exists(d):
                    pe.wait_ge(chosen_ready, m - 3)
                    wait(pe, base_ready, m - 4)
                    n = steps_of(d)
                    for t in range(n):
                        pe.matmul(ps_rank[:, t * E:(t + 1) * E], tri[:], chosen[:, t, :],
                                  start=True, stop=(t == 0), skip_group_check=True)
                        for s in range(t):
                            pe.matmul(ps_rank[:, t * E:(t + 1) * E], ones[:], chosen[:, s, :],
                                      start=False, stop=(s == t - 1), skip_group_check=True)
                    for t in range(n):
                        last = pe.matmul(ps_rank[:, TQ * E:(TQ + 1) * E], ones[:], chosen[:, t, :],
                                         start=(t == 0), stop=(t == n - 1), skip_group_check=True)
                    last.then_inc(rank_ready, 1)
                if exists(m):
                    pe.wait_ge(x_landed[q], 32 if isinstance(m, int) else 32 + x_iter(m, q))
                    for c in range(KC):
                        pe.matmul(ps_h[:], wm[:, c, :], xm[:, q, c, :], start=(c == 0), stop=False)
                    pe.matmul(ps_h[:], wt[:], xt[:, q, :], start=False, stop=True).then_inc(h_summed, 1)
                if exists(a):
                    pe.wait_ge(u_ready, m)
                    wait(pe, ut_copied, m - 1)
                    for t in range(steps_of(a)):
                        last = pe.transpose(ps_ut[:, t * 128:(t + 1) * 128], u_b[:, t, :], ident)
                    last.then_inc(ut_ready, 1)
                if exists(b):
                    pe.wait_ge(v_ready, m - 1)
                    wait(pe, row_copied, m - 2)
                    sv = HSLOT[slot(q, 2)]
                    n = steps_of(b)
                    for t in range(n):
                        pe.wait_ge(state_done, last_t(b) - (n - 1 - t))
                        o = ps_o[t // 2][:, (t % 2) * ROW:(t % 2 + 1) * ROW]
                        pe.matmul(o, v_t[:, sv, t, :], rhs_v[:], start=True, stop=False)
                        pe.matmul(o, states[:, t, 0, :], rhs_s[:, 0, :], start=False, stop=False)
                        last = pe.matmul(o, states[:, t, 1, :], rhs_s[:, 1, :], start=False, stop=True)
                    last.then_inc(out_ready, 1)
                if exists(a):
                    pe.wait_ge(ut_copied, m)
                    if exists(b):
                        pe.wait_ge(state_done, last_t(b))
                    n = steps_of(a) * B
                    rhs = u_t[:, 0:steps_of(a), :]
                    pe.matmul(ps_bur[:, 0:n], bt[:, 0, :], rhs, start=True, stop=True)
                    pe.matmul(ps_bui[:, 0:n], bt[:, 1, :], rhs, start=True, stop=True).then_inc(bu_ready, 1)

            iters = [None]

            def x_iter(m, q):
                return iters[0]

            for q in range(U):
                step(q + 1, q)
            with pe.Fori(1, NQ // U) as i:
                first = i * U
                iters[0] = i * 32
                for q in range(U):
                    step(first + (q + 1), q)
            for m in range(NQ + 1, NQ + 6):
                step(m, (m - 1) % U)

            def turn(k, p):
                pe.wait_ge(xn_ready, k + 1)
                wait(pe, xt_copied, k)
                for j in range(TJ):
                    last = pe.transpose(ps_xt[:, j * 128:(j + 1) * 128], xn[:, j, :], ident)
                last.then_inc(xt_ready, 1)

            def tile(k, p, landed, final):
                pe.wait_ge(xt_copied, k + 1)
                pe.wait_ge(tile_landed[p], landed)
                for c in range(FC):
                    wait(pe, gelu_done, k * FC + (c + 1 - FC))
                    pe.matmul(ps_g[c][:], w1_t[:, p, c, :], xn_t[:], start=True, stop=True).then_inc(up_ready, 1)
                if not final:
                    turn(k + 1, 1 - p)
                wait(pe, combined, k - 1)
                for j in range(TJ):
                    for c in range(FC):
                        if j == 0:
                            pe.wait_ge(gelu_done, k * FC + (c + 1))
                        last = pe.matmul(ps_y[p][:, j * 128:(j + 1) * 128], hidden[:, p, c, j * 128:(j + 1) * 128],
                                         w2_t[:, p, c, :], start=(c == 0), stop=(c == FC - 1))
                last.then_inc(y_ready, 1)

            turn(0, 0)
            for p in range(2):
                tile(p, p, 48, False)
            with pe.Fori(1, NT // 2 - 1) as i:
                landed = i * 48 + 48
                for p in range(2):
                    tile(i * 2 + p, p, landed, False)
            for p in range(2):
                tile(NT - 2 + p, p, 48 * (NT // 2), p == 1)

        @block.scalar
        def _(act):
            act.dma_start(vec[:], vecs).then_inc(vec_landed, 16)
            act.dma_start(bri[:], b_ri).then_inc(bc_landed, 16)
            act.dma_start(rhs_s[:, :, 0:HID], c_ph).then_inc(bc_landed, 16)
            act.dma_start(wg_sb[:], wg).then_inc(w_landed, 16)
            act.dma_start(chp[:], c_hp).then_inc(w_landed, 16)
            act.dma_start(wm[:], w_main).then_inc(w_landed, 16)
            act.dma_start(wt[:], w_tail).then_inc(w_landed, 16)
            act.dma_start(pos[:], posT).then_inc(w_landed, 16)
            act.wait_ge(vec_landed, 16)
            act.activation(lam[:, 0:1], vec[:, V_STEP:V_STEP + 1], ACT.Exp).then_inc(setup_act, 1)
            act.wait_ge(setup_act, 1)
            act.activation(lam[:, 1:2], vec[:, V_LR:V_LR + 1], ACT.Exp, scale=lam[:, 0:1]).then_inc(setup_act, 1)
            act.wait_ge(plan_step, 1)
            act.activation(lam[:, 8:10], lam[:, 6:8], ACT.Sin).then_inc(setup_act, 1)
            act.wait_ge(plan_step, 2)
            act.wait_ge(memsets_done, 1)
            act.activation(h_t[:, HSLOT[U - 1], 0, :], zeros[:], ACT.Identity, bias=lam[:, 20:21]).then_inc(h_copied, 1)

            def step(m, q):
                a, b, d = m - 1, m - 2, m - 4
                if exists(d):
                    n = steps_of(d)
                    act.wait_ge(scaled_ready, m - 3)
                    wait(act, gate_ready, m - 4)
                    act.activation(expd[:, 0:n, :], scaled[:, 0:n, :], ACT.Exp).then_inc(exp_ready, 1)
                if exists(a):
                    act.wait_ge(norm1, m)
                    act.wait_ge(hb_ready, m)
                    wait(act, ut_ready, m - 1)
                    for t in range(steps_of(a)):
                        last = act.activation(u_b[:, t, :], ps_ht[:, t * 128:(t + 1) * 128], ACT.Identity,
                                              bias=nmr1[:, t:t + 1], scale=rs1[:, t:t + 1])
                    last.then_inc(u_ready, 1)
                if exists(m):
                    act.wait_ge(h_summed, m)
                    wait(act, v_ready, m - 1)
                    for t in range(TQ):
                        col = TQ * (m - 1) + (t + 1)
                        bias = pos[:, col:col + 1] if isinstance(m, int) else pos[:, bass.ds(col, 1)]
                        last = act.activation(h_t[:, HSLOT[q], t, :], ps_h[:, t * 128:(t + 1) * 128], ACT.Identity,
                                              bias=bias)
                    last.then_inc(h_copied, 1)
                if exists(a):
                    act.wait_ge(ut_ready, m)
                    wait(act, bu_ready, m - 1)
                    wait(act, v_ready, m - 1)
                    n = steps_of(a)
                    act.activation(u_t[:, 0:n, :], ps_ut[:, 0:n * 128].rearrange("p (t b) -> p t b", t=n), ACT.Copy)\
                        .then_inc(ut_copied, 1)
                if exists(b):
                    act.wait_ge(out_ready, m - 1)
                    qs = slot(q, 2)
                    wait(act, rows_left, m - 7)
                    n = steps_of(b)
                    for g in range((n + 1) // 2):
                        w = min(2, n - 2 * g)
                        last = act.activation(rows[:, qs, 2 * g:2 * g + w, :],
                                              ps_o[g][:, 0:w * ROW].rearrange("p (t c) -> p t c", t=w), ACT.Copy)
                    last.then_inc(row_copied, 1)

            act.wait_ge(setup_dve, 2)
            for q in range(U):
                step(q + 1, q)
            with act.Fori(1, NQ // U) as i:
                first = i * U
                for q in range(U):
                    step(first + (q + 1), q)
            for m in range(NQ + 1, NQ + 6):
                step(m, (m - 1) % U)

            def tile(k, p):
                act.wait_ge(xt_ready, k + 1)
                wait(act, up_ready, k * FC)
                act.activation(xn_t[:], ps_xt[:], ACT.Copy).then_inc(xt_copied, 1)
                wait(act, y_ready, k - 1)
                for c in range(FC):
                    act.wait_ge(up_ready, k * FC + (c + 1))
                    act.activation(hidden[:, p, c, :], ps_g[c][:], ACT.Gelu).then_inc(gelu_done, 1)

            for p in range(2):
                tile(p, p)
            with act.Fori(1, NT // 2) as i:
                for p in range(2):
                    tile(i * 2 + p, p)

        @block.vector
        def _(dve):
            dve.memset(ones[:], 1.0)
            dve.memset(ones_mean[:], 1.0 / HID)
            dve.memset(eps_t[:], EPS)
            dve.memset(half_t[:], -0.5)
            dve.memset(neg_t[:], -1.0)
            dve.memset(four_t[:], float(TQ))
            dve.memset(one_e[:], 1.0)
            dve.memset(filler[:], 0.0)
            dve.memset(zeros[:], 0.0).then_inc(memsets_done, 1)

            chain = [0]

            def link(ins):
                chain[0] += 1
                ins.then_inc(setup_chain, 1)
                dve.wait_ge(setup_chain, chain[0])

            def col(n):
                return lam[:, n:n + 1]

            def tt(o, x, y, op):
                return dve.tensor_tensor(o, x, y, op)

            dve.wait_ge(memsets_done, 1)
            link(dve.memset(filler[:, :, LISTED - 1:LISTED], NOWHERE))
            dve.wait_ge(setup_act, 1)
            link(tt(col(2), vec[:, V_LI:V_LI + 1], col(0), ALU.mult))
            link(dve.tensor_scalar(col(3), col(2), 0.15915494309189535, 12582912.0, ALU.mult, ALU.add))
            link(dve.tensor_scalar(col(4), col(3), -12582912.0, None, ALU.add))
            link(dve.scalar_tensor_tensor(out=col(5), in0=col(4), scalar=-6.28125, in1=col(2), op0=ALU.mult, op1=ALU.add))
            link(dve.scalar_tensor_tensor(out=col(5), in0=col(4), scalar=-0.0019353071795864769, in1=col(5),
                                          op0=ALU.mult, op1=ALU.add))
            link(dve.tensor_scalar(col(6), col(5), 3.1415925, -3.1415925, ALU.min, ALU.max))
            dve.tensor_scalar(col(7), col(6), 0.5, None, ALU.mult).then_inc(plan_step, 1)
            dve.wait_ge(w_landed, 16 * 5)
            link(tt(col(20), vec[:, V_TOK:V_TOK + 1], pos[:, 0:1], ALU.add))
            dve.tensor_scalar(pos[:, 1:SEQ], pos[:, 1:SEQ], vec[:, V_B:V_B + 1], None, ALU.add).then_inc(plan_step, 1)
            dve.wait_ge(setup_act, 3)
            link(tt(col(10), col(9), col(9), ALU.mult))
            link(dve.tensor_scalar(col(11), col(10), -2.0, 1.0, ALU.mult, ALU.add))
            link(tt(col(12), col(1), col(11), ALU.mult))
            link(tt(col(13), col(1), col(8), ALU.mult))
            link(dve.tensor_scalar(col(14), col(13), -1.0, None, ALU.mult))
            link(dve.tensor_scalar(col(15), col(12), -1.0, None, ALU.add))
            lr, li = vec[:, V_LR:V_LR + 1], vec[:, V_LI:V_LI + 1]
            link(tt(col(16), lr, lr, ALU.mult))
            link(dve.scalar_tensor_tensor(out=col(16), in0=li, scalar=li, in1=col(16), op0=ALU.mult, op1=ALU.add))
            link(dve.reciprocal(col(17), col(16)))
            link(tt(col(18), col(13), li, ALU.mult))
            link(dve.scalar_tensor_tensor(out=col(18), in0=col(15), scalar=lr, in1=col(18), op0=ALU.mult, op1=ALU.add))
            link(tt(col(18), col(18), col(17), ALU.mult))
            link(tt(col(19), col(15), li, ALU.mult))
            link(dve.scalar_tensor_tensor(out=col(19), in0=col(13), scalar=lr, in1=col(19), op0=ALU.mult,
                                          op1=ALU.subtract))
            link(tt(col(19), col(19), col(17), ALU.mult))
            link(dve.tensor_scalar(col(21), col(19), -1.0, None, ALU.mult))
            dve.wait_ge(bc_landed, 32)
            link(dve.tensor_scalar(bbar[:, 0, :], bri[:, 0, :], col(18), None, ALU.mult))
            link(dve.scalar_tensor_tensor(out=bbar[:, 0, :], in0=bri[:, 1, :], scalar=col(21), in1=bbar[:, 0, :],
                                          op0=ALU.mult, op1=ALU.add))
            link(dve.tensor_scalar(bbar[:, 1, :], bri[:, 1, :], col(18), None, ALU.mult))
            link(dve.scalar_tensor_tensor(out=bbar[:, 1, :], in0=bri[:, 0, :], scalar=col(19), in1=bbar[:, 1, :],
                                          op0=ALU.mult, op1=ALU.add))
            dve.wait_ge(setup_pe, 1)
            dve.wait_ge(consts_landed, 16)
            tt(rhs_v[:, HID:ROW], wg_sb[:], ps_h[:, 0:E], ALU.subtract)
            dve.tensor_copy(rhs_v[:, 0:HID], ident)
            dve.tensor_copy(tri[:], cst[:, C_TRI:C_TRI + 128])
            dve.tensor_copy(base[:, 0, :], cst[:, C_BASE:C_BASE + E])
            dve.tensor_scalar(rhs_s[:, 0, 0:HID], rhs_s[:, 0, 0:HID], 2.0, None, ALU.mult)
            dve.tensor_scalar(rhs_s[:, 1, 0:HID], rhs_s[:, 1, 0:HID], -2.0, None, ALU.mult).then_inc(setup_dve, 1)
            dve.wait_ge(setup_pe, 2)
            dve.tensor_copy(bt[:], ps_ht[:, 0:256].rearrange("p (c h) -> p c h", c=2))
            dve.wait_ge(setup_pe, 3)
            dve.tensor_scalar(rhs_s[:, 0, HID:ROW], ps_ut[:, 0:E], 2.0, None, ALU.mult)
            dve.tensor_scalar(rhs_s[:, 1, HID:ROW], ps_ut[:, 64:64 + E], -2.0, None, ALU.mult).then_inc(setup_dve, 1)
            dve.wait_ge(setup_dve, 2)

            re_l, im_l, neg_im_l = col(12), col(13), col(14)
            d_col = vec[:, V_D:V_D + 1]

            def bc_e(x, n):
                return x.rearrange("p (t o) -> p t o", o=1).broadcast_to([128, n, E])

            def step(m, q):
                a, b, c3, c4 = m - 1, m - 2, m - 3, m - 4
                if exists(a):
                    dve.wait_ge(hb_ready, m)
                    n = steps_of(a)
                    for t in range(n):
                        last = dve.bn_stats(st1[:, t, :], ps_ht[:, t * 128:(t + 1) * 128])
                    last.then_inc(stats1_parts, 1)
                late = []
                if exists(a):
                    wait(dve, norm1, m - 1)
                    dve.wait_ge(stats1_parts, m)
                if exists(c4):
                    n4 = steps_of(c4)
                    qs4 = slot(q, 4)
                    k4 = m - 3
                    dve.wait_ge(rs2_ready, k4)
                    dve.wait_ge(below_ready, k4)
                    tt(scaled[:, 0:n4, :], below[:, 0:n4, :], bc_e(rs2[:, 0, 0:n4], n4), ALU.mult)\
                        .then_inc(scaled_ready, 1)
                if exists(a):
                    for t in range(steps_of(a)):
                        last = dve.bn_aggr(mv1[:, t, :], st1[:, t, :])
                    last.then_inc(moments1, 1)
                if exists(c4):
                    def r_place():
                        dve.wait_ge(rank_ready, k4)
                        wait(dve, base_ready, k4 - 1)
                        tt(place[:, 0:n4, :], ps_rank[:, 0:n4 * E].rearrange("p (t e) -> p t e", e=E),
                           base[:, 0, :].rearrange("p (o e) -> p o e", o=1).broadcast_to([128, n4, E]), ALU.add)\
                            .then_inc(place_ready, 1)

                    def r_base():
                        dve.wait_ge(place_ready, k4)
                        tt(base[:, 0, :], base[:, 0, :], ps_rank[:, TQ * E:(TQ + 1) * E], ALU.add)\
                            .then_inc(base_ready, 1)

                    def r_sum():
                        dve.wait_ge(exp_ready, k4)
                        dve.tensor_reduce(exp_sum[:, 0:n4], expd[:, 0:n4, :], AX, ALU.add).then_inc(sum_ready, 1)

                    def r_others():
                        dve.scalar_tensor_tensor(out=others[:, 0:n4, :], in0=chosen[:, 0:n4, :], scalar=0.0,
                                                 in1=expd[:, 0:n4, :], op0=ALU.is_equal, op1=ALU.mult)\
                            .then_inc(others_ready, 1)

                    def r_at():
                        tt(listed_at[:, 0:n4, :], place[:, 0:n4, :], chosen[:, 0:n4, :], ALU.mult)\
                            .then_inc(at_ready, 1)

                    def r_second():
                        dve.wait_ge(others_ready, k4)
                        dve.tensor_reduce(second[:, 0:n4], others[:, 0:n4, :], AX, ALU.max).then_inc(second_ready, 1)

                    def r_destf():
                        dve.wait_ge(at_ready, k4)
                        dve.tensor_reduce(dest_f[:, 0:n4], listed_at[:, 0:n4, :], AX, ALU.add).then_inc(destf_ready, 1)

                    def r_den():
                        dve.wait_ge(sum_ready, k4)
                        dve.wait_ge(second_ready, k4)
                        dve.scalar_tensor_tensor(out=gate_den[:, 0:n4], in0=exp_sum[:, 0:n4], scalar=GATE_EPS,
                                                 in1=second[:, 0:n4], op0=ALU.mult, op1=ALU.add).then_inc(den_ready, 1)

                    def r_dest():
                        dve.wait_ge(destf_ready, k4)
                        dve.tensor_copy(dest[:, qs4, 0:n4], dest_f[:, 0:n4]).then_inc(dest_ready, 1)

                    def r_den1():
                        dve.wait_ge(den_ready, k4)
                        dve.tensor_scalar(gate_den1[:, 0:n4], gate_den[:, 0:n4], 1.0, None, ALU.add)\
                            .then_inc(den1_ready, 1)

                    def r_gate():
                        dve.wait_ge(den1_ready, k4)
                        dve.reciprocal(rows[:, qs4, 0:n4, HID + 2], gate_den1[:, 0:n4]).then_inc(gate_ready, 1)

                    late = [(r_place, ), (r_base, ), (r_sum, r_at), (r_others, r_destf), (r_second, r_dest), (r_den, ),
                            (r_den1, ), (r_gate, )]

                early = []
                if exists(c3):
                    n3 = steps_of(c3)
                    qs3 = slot(q, 3)
                    k3 = m - 2
                    row3 = rows[:, qs3, 0:n3, :]

                    def s_stats():
                        dve.wait_ge(row_copied, k3)
                        for t in range(n3):
                            last = dve.bn_stats(st2[:, t, :], rows[:, qs3, t, 0:HID])
                        last.then_inc(stats2_parts, 1)

                    def s_top():
                        dve.tensor_reduce(top[:, 0:n3], row3[:, :, RAW:RAW + E], AX, ALU.max).then_inc(top_ready, 1)

                    def s_aggr():
                        for t in range(n3):
                            last = dve.bn_aggr(mv2[:, t, :], st2[:, t, :])
                        last.then_inc(moments2, 1)

                    def s_below():
                        dve.wait_ge(stats2_parts, k3)
                        wait(dve, nmr2_ready, k3 - 1)
                        dve.wait_ge(top_ready, k3)
                        tt(below[:, 0:n3, :], row3[:, :, RAW:RAW + E], bc_e(top[:, 0:n3], n3), ALU.subtract)\
                            .then_inc(below_ready, 1)

                    def s_key():
                        dve.wait_ge(below_ready, k3)
                        dve.scalar_tensor_tensor(out=key[:, 0:n3, :], in0=below[:, 0:n3, :], scalar=0.0,
                                                 in1=tie_weight[:, 0:n3, :], op0=ALU.is_equal, op1=ALU.mult)\
                            .then_inc(key_ready, 1)

                    def s_keytop():
                        dve.wait_ge(key_ready, k3)
                        dve.tensor_reduce(key_top[:, 0:n3], key[:, 0:n3, :], AX, ALU.max).then_inc(keytop_ready, 1)

                    def s_chosen():
                        dve.wait_ge(keytop_ready, k3)
                        tt(chosen[:, 0:n3, :], key[:, 0:n3, :], bc_e(key_top[:, 0:n3], n3), ALU.is_equal)\
                            .then_inc(chosen_ready, 1)

                    early = [s_stats, s_top, s_below, s_aggr]

                if exists(b):
                    dve.wait_ge(bu_ready, m - 1)
                    wait(dve, out_ready, m - 2)
                    if isinstance(b, int) and b == 0:
                        bu0 = [ps_bur, ps_bui]
                        for r in range(2):
                            last = dve.tensor_copy(states[:, TQ - 1, r, :], bu0[r][:, 0:B])
                        for r in range(2):
                            last = dve.tensor_copy(states[:, 0, r, :], bu0[r][:, 0:B])
                        last.then_inc(state_done, 1)
                    else:
                        for t in range(TQ):
                            T = last_t(b) - TQ + t
                            pv = (t - 1) % TQ
                            dd = decayed[:, t % 2, :, :]
                            dve.wait_ge(state_done, T)
                            for r, bank_r in enumerate((ps_bur, ps_bui)):
                                last = dve.scalar_tensor_tensor(
                                    out=dd[:, r, :], in0=states[:, pv, r, :], scalar=re_l,
                                    in1=bank_r[:, t * B:(t + 1) * B], op0=ALU.mult, op1=ALU.add)
                            last.then_inc(decay_done, 1)
                            if late:
                                for f in late.pop(0):
                                    f()
                            dve.wait_ge(decay_done, T)
                            dve.scalar_tensor_tensor(out=states[:, t, 0, :], in0=states[:, pv, 1, :], scalar=neg_im_l,
                                                     in1=dd[:, 0, :], op0=ALU.mult, op1=ALU.add)
                            dve.scalar_tensor_tensor(out=states[:, t, 1, :], in0=states[:, pv, 0, :], scalar=im_l,
                                                     in1=dd[:, 1, :], op0=ALU.mult, op1=ALU.add)\
                                .then_inc(state_done, 1)
                            if late:
                                for f in late.pop(0):
                                    f()
                for fs in late:
                    for f in fs:
                        f()
                for f in early:
                    f()
                if exists(a):
                    n = steps_of(a)
                    sv = HSLOT[slot(q, 1)]
                    dve.wait_ge(ut_copied, m)
                    wait(dve, out_ready, m - 2)
                    if exists(c3):
                        s_key()
                    dve.scalar_tensor_tensor(out=v_t[:, sv, 0:n, :], in0=u_t[:, 0:n, :], scalar=d_col,
                                             in1=h_t[:, sv, 0:n, :], op0=ALU.mult, op1=ALU.add).then_inc(v_ready, 1)
                elif exists(c3):
                    s_key()
                if exists(c3):
                    s_keytop()
                    s_chosen()

            for_steps(dve, step)

            pchain = [2]

            def plink(ins):
                pchain[0] += 1
                ins.then_inc(plan_step, 1)
                dve.wait_ge(plan_step, pchain[0])

            dve.wait_ge(base_ready, NQ + 1)
            cst0 = cst[0:1, :]
            plink(tt(count[:], base[0:1, 0, :], cst0[:, C_BASE:C_BASE + E], ALU.subtract))
            plink(tt(cmp_t[:], count[:].rearrange("o (e j) -> o e j", j=1).broadcast_to([1, E, MAXT]),
                     cst0[:, C_GRID:C_GRID + MAXT].rearrange("o (e j) -> o e j", e=1).broadcast_to([1, E, MAXT]),
                     ALU.is_gt))
            plink(dve.tensor_reduce(ntile[:], cmp_t[:], AX, ALU.add))
            plink(dve.tensor_tensor_scan(cum[:], one_e[:], ntile[:], 0.0, ALU.mult, ALU.add))
            grid_k = cst0[:, C_K:C_K + NT]
            plink(tt(passed[:], grid_k.rearrange("o (k e) -> o k e", e=1).broadcast_to([1, NT, E]),
                     cum[:].rearrange("o (k e) -> o k e", k=1).broadcast_to([1, NT, E]), ALU.is_ge))
            plink(dve.tensor_reduce(expert_f[:], passed[:], AX, ALU.add))
            plink(tt(before[:], passed[:], ntile[:].rearrange("o (k e) -> o k e", k=1).broadcast_to([1, NT, E]),
                     ALU.mult))
            plink(dve.tensor_reduce(before_f[:], before[:], AX, ALU.add))
            plink(tt(start_f[:, 0, :], grid_k, before_f[:], ALU.subtract))
            plink(dve.tensor_scalar(start_f[:, 1, :], expert_f[:], float(REGION), None, ALU.mult))
            plink(dve.scalar_tensor_tensor(out=start_f[:, 2, :], in0=start_f[:, 0, :], scalar=float(TILE),
                                           in1=start_f[:, 1, :], op0=ALU.mult, op1=ALU.add))
            plink(dve.tensor_scalar(start_i[:], start_f[:, 2, :], float(E * REGION), None, ALU.min))
            plink(dve.tensor_scalar(expert_i[:], expert_f[:], float(E - 1), None, ALU.min))
            dve.tensor_copy(base_i[:], base[0:1, 0, :]).then_inc(plan_ready, 1)
            dve.wait_ge(w1_loaded, 16)
            for e in range(E):
                last = dve.tensor_scalar(w1_out[:, e, :].rearrange("d (c p) -> d p c", c=FC),
                                         w1_in[:, e, :].rearrange("d (p c) -> d p c", c=FC),
                                         vec[:, V_GAMMA:V_GAMMA + 1], None, ALU.mult)
            last.then_inc(w1_scaled_ready, 1)

            def normalise(k, p, landed):
                dve.wait_ge(tile_landed[p], landed)
                wait(dve, xt_ready, k)
                for j in range(TJ):
                    last = dve.tensor_scalar(xn[:, j, :], lt[:, p, j, 0:HID], lt[:, p, j, HID:HID + 1],
                                             lt[:, p, j, HID + 1:HID + 2], ALU.mult, ALU.add)
                last.then_inc(xn_ready, 1)

            def combine(k, p, stored_before):
                wait(dve, stored[p], stored_before)
                dve.tensor_copy(place_i[:, p, :], lt[:, p, :, HID + 3]).then_inc(placei_ready, 1)
                dve.wait_ge(y_ready, k + 1)
                for j in range(TJ):
                    last = dve.scalar_tensor_tensor(out=res[:, p, j, :], in0=ps_y[p][:, j * 128:(j + 1) * 128],
                                                    scalar=lt[:, p, j, HID + 2:HID + 3], in1=lt[:, p, j, 0:HID],
                                                    op0=ALU.mult, op1=ALU.add)
                last.then_inc(combined, 1)

            normalise(0, 0, 48)
            normalise(1, 1, 48)
            combine(0, 0, 0)
            normalise(2, 0, 96)
            combine(1, 1, 0)
            normalise(3, 1, 96)
            combine(2, 0, 16 * TJ)
            with dve.Fori(2, NT // 2) as i:
                landed = i * 48 + 48
                stored_before = i * (16 * TJ)
                normalise(i * 2, 0, landed)
                combine(i * 2 - 1, 1, stored_before - 16 * TJ)
                normalise(i * 2 + 1, 1, landed)
                combine(i * 2, 0, stored_before)
            combine(NT - 1, 1, 16 * TJ * (NT // 2 - 1))

        @block.gpsimd
        def _(pool):
            def tt(o, x, y, op):
                return pool.tensor_tensor(o, x, y, op)

            pool.wait_ge(memsets_done, 1)
            pool.wait_ge(vec_landed, 16)
            pool.tensor_copy(out_row[:, 0:1], vec[:, V_IMG:V_IMG + 1]).then_inc(outrow_ready, 1)

            def step(m, q):
                a, c3, c5 = m - 1, m - 3, m - 5
                if exists(a):
                    n = steps_of(a)
                    pool.wait_ge(moments1, m)
                    wait(pool, u_ready, m - 1)
                    tt(ve1[:, 0:n], mv1[:, 0:n, 1], eps_t[:, 0:n], ALU.add).then_inc(ve1_ready, 1)
                    tt(nm1[:, 0:n], mv1[:, 0:n, 0], neg_t[:, 0:n], ALU.mult).then_inc(nm1_ready, 1)
                    pool.wait_ge(ve1_ready, m)
                    tt(rs1[:, 0:n], ve1[:, 0:n], half_t[:, 0, 0:n], ALU.pow).then_inc(rs1_ready, 1)
                    pool.wait_ge(rs1_ready, m)
                    pool.wait_ge(nm1_ready, m)
                    tt(nmr1[:, 0:n], nm1[:, 0:n], rs1[:, 0:n], ALU.mult).then_inc(norm1, 1)
                j = m - 6
                if exists(j):
                    qs = slot(q, 6)
                    own = 16 if qs == U - 1 else 0
                    if isinstance(m, int):
                        pool.wait_ge(listed[qs], 16 * TQ * ((j - 1) // U + 1) + own)
                    else:
                        pool.wait_ge(listed[qs], iters[0] + ((16 * TQ if q == U - 1 else 0) + own))
                    pool.sem_inc(rows_left, 1)
                if exists(c5):
                    n = steps_of(c5)
                    qs = slot(q, 5)
                    pool.wait_ge(gate_ready, m - 4)
                    pool.wait_ge(dest_ready, m - 4)
                    pool.wait_ge(meta_ready, m - 4)
                    pool.sem_inc(pool_passed, 1)
                    for t in range(n):
                        pool.indirect_dma_start(
                            out=lists, out_offset=bass.IndirectOffsetOnAxis(ap=dest[:, qs, t:t + 1], axis=0),
                            in_=rows[:, qs, t, 0:LISTED], in_offset=None,
                            bounds_check=E * REGION - 1, oob_is_err=True).then_inc(listed[qs], 16)
                if exists(c3):
                    n = steps_of(c3)
                    qs = slot(q, 3)
                    k = m - 2
                    pool.wait_ge(moments2, k)
                    wait(pool, scaled_ready, k - 1)
                    tt(ve2[:, 0, 0:n], mv2[:, 0:n, 1], eps_t[:, 0:n], ALU.add).then_inc(ve2a_ready, 1)
                    tt(nm2[:, 0:n], mv2[:, 0:n, 0], neg_t[:, 0:n], ALU.mult).then_inc(nm2_ready, 1)
                    pool.wait_ge(ve2a_ready, k)
                    tt(ve2[:, 1, 0:n], ve2[:, 0, 0:n], eps_t[:, 0:n], ALU.mult).then_inc(ve2b_ready, 1)
                    pool.wait_ge(ve2b_ready, k)
                    tt(ve2[:, 1, 0:n], ve2[:, 1, 0:n], mv2[:, 0:n, 1], ALU.add).then_inc(ve2c_ready, 1)
                    pool.wait_ge(ve2c_ready, k)
                    tt(rs2[:, :, 0:n], ve2[:, :, 0:n], half_t[:, :, 0:n], ALU.pow).then_inc(rs2_ready, 1)
                    pool.wait_ge(rs2_ready, k)
                    pool.wait_ge(below_ready, k)
                    pool.wait_ge(nm2_ready, k)
                    tt(rows[:, qs, 0:n, HID + 1], nm2[:, 0:n], rs2[:, 1, 0:n], ALU.mult).then_inc(nmr2_ready, 1)
                    pool.tensor_copy(rows[:, qs, 0:n, HID], rs2[:, 1, 0:n])
                    pool.wait_ge(outrow_ready, k)
                    pool.sem_inc(pool_passed, 1)
                    pool.tensor_copy(rows[:, qs, 0:n, HID + 3], out_row[:, 0:n]).then_inc(meta_ready, 1)
                    pool.wait_ge(meta_ready, k)
                    if isinstance(m, int) and c3 == 0:
                        for t in range(TQ):
                            last = pool.tensor_scalar(out_row[:, t:t + 1], vec[:, V_IMG:V_IMG + 1], float(t + 1), None,
                                                      ALU.add)
                        last.then_inc(outrow_ready, 1)
                    else:
                        tt(out_row[:], out_row[:], four_t[:], ALU.add).then_inc(outrow_ready, 1)

            iters = [None]
            for q in range(U):
                step(q + 1, q)
            with pool.Fori(1, NQ // U) as i:
                first = i * U
                iters[0] = i * (16 * TQ)
                for q in range(U):
                    step(first + (q + 1), q)
            for m in range(NQ + 1, NQ + 6):
                step(m, (m - 1) % U)

            with pool.Fori(0, NT // 2) as i:
                for p in range(2):
                    k = i * 2 + p
                    pool.wait_ge(placei_ready, k + 1)
                    pool.wait_ge(combined, k + 1)
                    pool.sem_inc(pool_passed, 1)
                    for j in range(TJ):
                        pool.indirect_dma_start(
                            out=out, out_offset=bass.IndirectOffsetOnAxis(ap=place_i[:, p, j:j + 1], axis=0),
                            in_=res[:, p, j, :], in_offset=None,
                            bounds_check=NTOK - 1, oob_is_err=False).then_inc(stored[p], 16)


def kernel(**inputs):
    import numpy as np
    import concourse.bacc as bacc
    from concourse.bass_utils import run_bass_kernel_spmd

    get = {k: np.asarray(v) for k, v in inputs.items()}
    x = get["x"].reshape(B, 3, GRID, 14, GRID, 14).transpose(2, 4, 1, 3, 5, 0).reshape(NQ, TQ, IN_DIM, B)
    x = x.transpose(0, 2, 1, 3)
    w = get["L0_tok_W"].T
    bm, cm = get["L0_attn_B"], get["L0_attn_C"]
    images = np.arange(B, dtype=np.float32) * SEQ
    consts = np.zeros((128, C_END), np.float32)
    consts[:, C_ID:C_ID + 128] = np.eye(128)
    consts[:, C_TRI:C_TRI + 128] = np.triu(np.ones((128, 128)), 1)
    consts[:, C_WT:C_WT + TQ * E] = np.tile(np.arange(E, 0, -1), TQ)
    consts[:, C_BASE:C_BASE + E] = np.arange(E) * REGION
    consts[:, C_GRID:C_GRID + MAXT] = np.arange(MAXT) * TILE
    consts[:, C_K:C_K + NT] = np.arange(NT)
    arrays = {
        "x_main": x[:, :KC * 128].reshape(NQ, KC, 128, TQ * B).transpose(0, 2, 1, 3),
        "x_tail": x[:, KC * 128:].reshape(NQ, KT, TQ * B),
        "w_main": w[:KC * 128].reshape(KC, 128, HID).transpose(1, 0, 2),
        "w_tail": w[KC * 128:],
        "vecs": np.stack([get["L0_attn_lambda_real"], get["L0_attn_lambda_imag"], get["L0_attn_log_step"][:, 0],
                          get["L0_attn_D"], get["L0_tok_b"], get["L0_tok_token"][0], get["L0_ffn_gamma"], images], 1),
        "posT": get["L0_tok_pos"].T,
        "b_ri": bm.transpose(0, 2, 1),
        "c_hp": cm.transpose(0, 2, 1),
        "c_ph": cm.transpose(1, 2, 0),
        "wg": get["L0_ffn_w_gating"],
        "w1": get["L0_ffn_w1"],
        "w2": get["L0_ffn_w2"],
        "consts": consts,
    }
    nc = bacc.Bacc("TRN2", target_bir_lowering=False, num_devices=1)
    args = []
    for name in arrays:
        a = arrays[name] = np.ascontiguousarray(arrays[name])
        args.append(nc.dram_tensor(name, a.shape, mybir.dt.from_np(a.dtype), kind="ExternalInput").ap())
    args.append(nc.dram_tensor("out", (NTOK, HID), F32, kind="ExternalOutput").ap())
    build(nc, *args)
    r = run_bass_kernel_spmd(nc, [arrays], core_ids=[0])
    return r.results[0]["out"].reshape(B, SEQ, HID)
```

```python
from contextlib import ExitStack

import concourse.bass as bass
from concourse import mybir

ALU = mybir.AluOpType
ACT = mybir.ActivationFunctionType
AX = mybir.AxisListType.X
F32 = mybir.dt.float32
F32R = mybir.dt.float32r
BF16 = mybir.dt.bfloat16
I32 = mybir.dt.int32
U32 = mybir.dt.uint32

B = 128
HID = 128
GRID = 14
IN_DIM = 3 * 14 * 14
SEQ = GRID * GRID + 1
KC = IN_DIM // 128
KT = IN_DIM - KC * 128
TQ = 4
NQ = (SEQ - 1) // TQ
U = 7
E = 6
FF = 512
FC = FF // 128
EPS = 1e-5
GATE_EPS = 1e-9
CAPACITY = max(min(SEQ, int(SEQ * 6.0 / E)), 4)
assert CAPACITY == SEQ and NQ % U == 0

NTOK = B * SEQ
TILE = 512
TJ = TILE // 128
REGION = NTOK + TILE
NT = (NTOK + E * (TILE - 1)) // TILE
V = 5
NT += -NT % V
LISTED = 132
RAW = HID
ROW = HID + E
NOWHERE = float(NTOK + 1000)
MAXT = (NTOK + TILE - 1) // TILE

V_LR, V_LI, V_STEP, V_D, V_B, V_TOK, V_GAMMA, V_IMG = range(8)
C_ID, C_TRI, C_WT = 0, 128, 256
C_BASE = C_WT + TQ * E
C_GRID = C_BASE + E
C_K = C_GRID + MAXT
C_END = C_K + NT


def build(nc, x_main, x_tail, w_main, w_tail, vecs, posT, b_ri, c_hp, c_ph, wg, w1, w2, consts, out):
    with ExitStack() as ctx:
        def sb(name, shape, dt=F32):
            return ctx.enter_context(nc.sbuf_tensor(name, shape, dt))

        def sem(name):
            return ctx.enter_context(nc.semaphore(name))

        def psum(name, *shape):
            return ctx.enter_context(nc.psum_tensor(name, [128, *shape], F32))

        ps_h, ps_ht, ps_ut, ps_bu = psum("ps_h", 512), psum("ps_ht", 512), psum("ps_ut", 512), psum("ps_bu", 2, 512)
        ps_o = [psum("ps_o0", 512), psum("ps_o1", 512)]
        ps_rank = psum("ps_rank", 512)
        ps_xt, ps_g = ps_h, [ps_ht[:], ps_ut[:], ps_bu[:, 0, :], ps_bu[:, 1, :]]
        ps_yt, ps_y = ps_o

        lists = nc.dram_tensor("lists", [E * REGION + TILE, LISTED], F32).ap()
        w_split = nc.dram_tensor("w_split", [E * HID, 4 * FF], F32).ap()

        cst = sb("cst", [128, C_END])
        ident = cst[:, C_ID:C_ID + 128]
        tie_weight = cst[:, C_WT:C_WT + TQ * E].rearrange("p (t e) -> p t e", e=E)
        vec = sb("vec", [128, 8])
        pos = sb("pos", [128, SEQ])
        wm = sb("wm", [128, KC, HID])
        wt = sb("wt", [KT, HID])
        bri = sb("bri", [128, 2, HID])
        chp = sb("chp", [128, 2, HID])
        wg_sb = sb("wg_sb", [128, E])
        lam = sb("lam", [128, 24])
        bbar = sb("bbar", [128, 2, HID])
        bt = sb("bt", [128, 2, HID])
        rhs_v = sb("rhs_v", [128, ROW])
        rhs_s = sb("rhs_s", [128, 2, ROW])
        tri = sb("tri", [128, 128], BF16)
        ones = sb("ones", [128, 128], BF16)
        ones_mean = sb("ones_mean", [128, 128])
        zeros = sb("zeros", [128, 128])
        eps_t = sb("eps_t", [128, TQ])
        half_t = sb("half_t", [128, 2, TQ])
        neg_t = sb("neg_t", [128, TQ])
        four_t = sb("four_t", [128, TQ])
        xm = sb("xm", [128, U, KC, TQ * B])
        xt = sb("xt", [KT, U, TQ * B])
        h_t = sb("h_t", [128, 3, TQ, B])
        u_b = sb("u_b", [128, TQ, HID])
        u_t = sb("u_t", [128, TQ, B])
        v_t = sb("v_t", [128, 3, TQ, B])
        states = sb("states", [128, TQ, 2, B])
        decayed = sb("decayed", [128, 2, 2, B])
        st1 = sb("st1", [128, TQ, 6])
        mv1 = sb("mv1", [128, TQ, 2])
        ve1 = sb("ve1", [128, TQ])
        rs1 = sb("rs1", [128, TQ])
        nm1 = sb("nm1", [128, TQ])
        nmr1 = sb("nmr1", [128, TQ])
        rows = sb("rows", [128, U, TQ, ROW])
        st2 = sb("st2", [128, TQ, 6])
        mv2 = sb("mv2", [128, TQ, 2])
        ve2 = sb("ve2", [128, 2, TQ])
        rs2 = sb("rs2", [128, 2, TQ])
        nm2 = sb("nm2", [128, TQ])
        out_row = sb("out_row", [128, TQ])
        top = sb("top", [128, TQ])
        below = sb("below", [128, TQ, E])
        key = sb("key", [128, TQ, E])
        key_top = sb("key_top", [128, TQ])
        chosen = sb("chosen", [128, TQ, E], BF16)
        scaled = sb("scaled", [128, TQ, E])
        expd = sb("expd", [128, TQ, E])
        exp_sum = sb("exp_sum", [128, TQ])
        others = sb("others", [128, TQ, E])
        second = sb("second", [128, TQ])
        gate_den = sb("gate_den", [128, TQ])
        gate_den1 = sb("gate_den1", [128, TQ])
        place = sb("place", [128, TQ, E])
        listed_at = sb("listed_at", [128, TQ, E])
        dest_f = sb("dest_f", [128, TQ])
        dest = sb("dest", [128, U, TQ], U32)
        base = sb("base", [128, 2, E])
        filler = sb("filler", [128, TJ, LISTED])
        count = sb("count", [1, E])
        cmp_t = sb("cmp_t", [1, E, MAXT])
        ntile = sb("ntile", [1, E])
        one_e = sb("one_e", [1, E])
        cum = sb("cum", [1, E])
        passed = sb("passed", [1, NT, E])
        expert_f = sb("expert_f", [1, NT])
        before = sb("before", [1, NT, E])
        before_f = sb("before_f", [1, NT])
        start_f = sb("start_f", [1, 3, NT])
        start_i = sb("start_i", [1, NT], I32)
        weights_f = sb("weights_f", [1, NT])
        weights_i = sb("weights_i", [1, NT], I32)
        base_i = sb("base_i", [1, E], I32)
        raw = sb("raw", [128, 2, 2, FF])
        w1_full = sb("w1_full", [128, FF])
        split = sb("split", [128, 4, FF], F32R)
        patches = xm[:].rearrange("p u c n -> p (u c n)")
        used = [0]

        def in_patches(n, pattern, **sizes):
            used[0] += n
            assert used[0] <= U * KC * TQ * B
            return patches[:, used[0] - n:used[0]].rearrange(pattern, **sizes)

        lt = in_patches(V * TJ * LISTED, "p (v j c) -> p v j c", v=V, j=TJ)
        xn = in_patches(TJ * HID, "p (j c) -> p j c", j=TJ)
        full = in_patches(FC * TILE, "p (c s) -> p c s", c=FC)
        y_t = in_patches(TILE, "p (o s) -> p o s", o=1)[:, 0, :]
        res = in_patches(V * TJ * HID, "p (v j c) -> p v j c", v=V, j=TJ)
        w_t = sb("w_t", [128, 3, 4, FC, 128], F32R)
        xn_t = sb("xn_t", [128, 2, TILE], F32R)
        hidden = sb("hidden", [128, 2, FC, TILE], F32R)
        place_i = sb("place_i", [128, V, TJ], U32)

        consts_landed, vec_landed, w_landed = sem("consts_landed"), sem("vec_landed"), sem("w_landed")
        bc_landed = sem("bc_landed")
        pool_passed = sem("pool_passed")
        memsets_done, setup_dve, setup_act, setup_pe, setup_chain = (
            sem("memsets_done"), sem("setup_dve"), sem("setup_act"), sem("setup_pe"), sem("setup_chain"))
        x_landed = [sem(f"x_landed{q}") for q in range(U)]
        h_summed, h_copied = sem("h_summed"), sem("h_copied")
        hb_ready, moments1, stats1_parts = sem("hb_ready"), sem("moments1"), sem("stats1_parts")
        ve1_ready, nm1_ready, rs1_ready, norm1 = sem("ve1_ready"), sem("nm1_ready"), sem("rs1_ready"), sem("norm1")
        u_ready, ut_ready, ut_copied, v_ready = sem("u_ready"), sem("ut_ready"), sem("ut_copied"), sem("v_ready")
        bu_ready = sem("bu_ready")
        decay_done, state_done = sem("decay_done"), sem("state_done")
        out_ready, row_copied = sem("out_ready"), sem("row_copied")
        stats2_parts, moments2 = sem("stats2_parts"), sem("moments2")
        ve2a_ready, ve2b_ready, ve2c_ready = sem("ve2a_ready"), sem("ve2b_ready"), sem("ve2c_ready")
        rs2_ready, nm2_ready, nmr2_ready = sem("rs2_ready"), sem("nm2_ready"), sem("nmr2_ready")
        outrow_ready, meta_ready = sem("outrow_ready"), sem("meta_ready")
        top_ready, below_ready, key_ready, keytop_ready, chosen_ready = (
            sem("top_ready"), sem("below_ready"), sem("key_ready"), sem("keytop_ready"), sem("chosen_ready"))
        scaled_ready, exp_ready, sum_ready, others_ready, second_ready = (
            sem("scaled_ready"), sem("exp_ready"), sem("sum_ready"), sem("others_ready"), sem("second_ready"))
        den_ready, den1_ready, gate_ready = sem("den_ready"), sem("den1_ready"), sem("gate_ready")
        rank_ready, place_ready, base_ready, at_ready, destf_ready, dest_ready = (
            sem("rank_ready"), sem("place_ready"), sem("base_ready"), sem("at_ready"), sem("destf_ready"),
            sem("dest_ready"))
        listed = [sem(f"listed{q}") for q in range(U)]
        rows_left = sem("rows_left")
        plan_step, plan_ready, filled = sem("plan_step"), sem("plan_ready"), sem("filled")
        raw_landed = [sem(f"raw_landed{p}") for p in range(2)]
        w_high, w_low, w_stored = sem("w_high"), sem("w_low"), sem("w_stored")
        tile_landed = [sem(f"tile_landed{v}") for v in range(V)]
        w_tile_landed = [sem(f"w_tile_landed{v}") for v in range(V)]
        xn_ready, xt_ready, xth_ready, xtl_ready = sem("xn_ready"), sem("xt_ready"), sem("xth_ready"), sem("xtl_ready")
        up_ready, gelu_done, low_done = sem("up_ready"), sem("gelu_done"), sem("low_done")
        yt_ready, yt_copied, y_ready, combined, placei_ready = (
            sem("yt_ready"), sem("yt_copied"), sem("y_ready"), sem("combined"), sem("placei_ready"))
        stored = [sem(f"stored{v}") for v in range(V)]
        results_left = sem("results_left")

        block = ctx.enter_context(nc.Block())

        def wait(eng, s, value):
            if not (isinstance(value, int) and value <= 0):
                eng.wait_ge(s, value)

        def exists(m):
            return not isinstance(m, int) or 0 <= m <= NQ

        def steps_of(m):
            return 1 if isinstance(m, int) and m == 0 else TQ

        def last_t(m):
            return TQ * m + 1

        HSLOT = [0, 1, 0, 1, 0, 1, 2]
        WSLOT = [0, 1, 0, 1, 2]

        def for_tiles(eng, step):
            for v in range(V):
                step(v, v)
            with eng.Fori(1, NT // V - 1) as i:
                first = i * V
                for v in range(V):
                    step(first + v, v, i)
            for v in range(V):
                step(NT - V + v, v)

        def for_steps(eng, step):
            for q in range(U):
                step(q + 1, q)
            with eng.Fori(1, NQ // U) as i:
                first = i * U
                for q in range(U):
                    step(first + (q + 1), q)
            for m in range(NQ + 1, NQ + 6):
                step(m, (m - 1) % U)

        def slot(q, lag):
            return (q - lag) % U

        @block.sync
        def _(sp):
            def load(m, q):
                wait(sp, h_summed, m - U)
                ix = m - 1
                sp.dma_start(xm[:, q, :, :], x_main[ix] if isinstance(m, int) else
                             x_main[bass.ds(ix, 1)].rearrange("o p c n -> (o p) c n")).then_inc(x_landed[q], 16)
                sp.dma_start(xt[:, q, :], x_tail[ix] if isinstance(m, int) else
                             x_tail[bass.ds(ix, 1)].rearrange("o p n -> (o p) n")).then_inc(x_landed[q], 16)

            def store_split(e):
                sp.wait_ge(w_low, e + 1)
                sp.dma_start(w_split[e * HID:(e + 1) * HID, :],
                             split[:].bitcast(F32).rearrange("p s f -> p (s f)")).then_inc(w_stored, 16)

            sp.dma_start(cst[:], consts).then_inc(consts_landed, 16)
            for q in range(U):
                load(q + 1, q)
            for e in range(E):
                wait(sp, w_low, e - 1)
                sp.dma_start(raw[:, e % 2, 0, :], w1[e]).then_inc(raw_landed[e % 2], 16)
                sp.dma_start(raw[:, e % 2, 1, :], w2[e].rearrange("(p c) d -> p (c d)", c=FC))\
                    .then_inc(raw_landed[e % 2], 16)
                if e:
                    store_split(e - 1)
            store_split(E - 1)
            with sp.Fori(1, NQ // U) as i:
                first = sp.snap(i * U)
                for q in range(U):
                    load(first + (q + 1), q)

            sp.wait_ge(plan_ready, 1)
            for e in range(E):
                end = sp.value_load(base_i[0:1, e:e + 1], min_val=e * REGION, max_val=e * REGION + NTOK)
                sp.dma_start(lists[bass.ds(end, TILE), :].rearrange("(j p) c -> p j c", p=128), filler[:])\
                    .then_inc(filled, 16)
            sp.dma_start(lists[E * REGION:E * REGION + TILE, :].rearrange("(j p) c -> p j c", p=128), filler[:])\
                .then_inc(filled, 16)
            sp.wait_ge(filled, 16 * (E + 1))
            sp.wait_ge(w_stored, 16 * E)
            for q in range(U):
                sp.wait_ge(listed[q], 16 * TQ * (NQ // U) + (16 if q == U - 1 else 0))

            def load_tile(k, v, i=0):
                at = slice(k, k + 1) if isinstance(k, int) else bass.ds(k, 1)
                row = sp.value_load(start_i[0:1, at], min_val=0, max_val=E * REGION)
                split_row = sp.value_load(weights_i[0:1, at], min_val=0, max_val=(E - 1) * HID)
                wait(sp, combined, k - (V - 1))
                sp.dma_start(lt[:, v, :, :], lists[bass.ds(row, TILE), :].rearrange("(j p) c -> p j c", p=128))\
                    .then_inc(tile_landed[v], 16)
                wait(sp, yt_ready, k - 1)
                sp.dma_start(w_t[:, WSLOT[v]].rearrange("p s c f -> p (s c f)").bitcast(F32),
                             w_split[bass.ds(split_row, HID), :]).then_inc(w_tile_landed[v], 16)

            for_tiles(sp, load_tile)
            for v in range(V):
                sp.wait_ge(stored[v], 16 * TJ * (NT // V))

        @block.tensor
        def _(pe):
            pe.wait_ge(w_landed, 16 * 5)
            pe.wait_ge(memsets_done, 1)
            pe.matmul(ps_h[:, 0:E], ones_mean[:], wg_sb[:], start=True, stop=True).then_inc(setup_pe, 1)
            pe.wait_ge(consts_landed, 16)
            pe.wait_ge(setup_dve, 1)
            for c in range(2):
                last = pe.transpose(ps_ht[:, c * 128:(c + 1) * 128], bbar[:, c, :], ident)
            last.then_inc(setup_pe, 1)
            for c in range(2):
                last = pe.matmul(ps_ut[:, c * 64:c * 64 + E], chp[:, c, :], rhs_v[:, HID:ROW], start=True, stop=True)
            last.then_inc(setup_pe, 1)

            def step(m, q):
                a, b = m - 1, m - 2
                if exists(a):
                    pe.wait_ge(h_copied, m)
                    wait(pe, u_ready, m - 1)
                    if isinstance(m, int) and m == 1:
                        pe.wait_ge(setup_dve, 2)
                    for t in range(steps_of(a)):
                        last = pe.transpose(ps_ht[:, t * 128:(t + 1) * 128], h_t[:, HSLOT[slot(q, 1)], t, :], ident)
                    last.then_inc(hb_ready, 1)
                d = m - 4
                if exists(d):
                    pe.wait_ge(chosen_ready, m - 3)
                    wait(pe, base_ready, m - 4)
                    n = steps_of(d)
                    for t in range(n):
                        pe.matmul(ps_rank[:, t * E:(t + 1) * E], tri[:], chosen[:, t, :],
                                  start=True, stop=(t == 0), skip_group_check=True)
                        for s in range(t):
                            pe.matmul(ps_rank[:, t * E:(t + 1) * E], ones[:], chosen[:, s, :],
                                      start=False, stop=(s == t - 1), skip_group_check=True)
                    for t in range(n):
                        last = pe.matmul(ps_rank[:, TQ * E:(TQ + 1) * E], ones[:], chosen[:, t, :],
                                         start=(t == 0), stop=(t == n - 1), skip_group_check=True)
                    last.then_inc(rank_ready, 1)
                if exists(m):
                    pe.wait_ge(x_landed[q], 32 if isinstance(m, int) else 32 + x_iter(m, q))
                    for c in range(KC):
                        pe.matmul(ps_h[:], wm[:, c, :], xm[:, q, c, :], start=(c == 0), stop=False)
                    pe.matmul(ps_h[:], wt[:], xt[:, q, :], start=False, stop=True).then_inc(h_summed, 1)
                if exists(a):
                    pe.wait_ge(u_ready, m)
                    wait(pe, ut_copied, m - 1)
                    for t in range(steps_of(a)):
                        last = pe.transpose(ps_ut[:, t * 128:(t + 1) * 128], u_b[:, t, :], ident)
                    last.then_inc(ut_ready, 1)
                if exists(b):
                    pe.wait_ge(v_ready, m - 1)
                    wait(pe, row_copied, m - 2)
                    sv = HSLOT[slot(q, 2)]
                    n = steps_of(b)
                    for t in range(n):
                        pe.wait_ge(state_done, last_t(b) - (n - 1 - t))
                        o = ps_o[t // 2][:, (t % 2) * ROW:(t % 2 + 1) * ROW]
                        pe.matmul(o, v_t[:, sv, t, :], rhs_v[:], start=True, stop=False)
                        pe.matmul(o, states[:, t, 0, :], rhs_s[:, 0, :], start=False, stop=False)
                        last = pe.matmul(o, states[:, t, 1, :], rhs_s[:, 1, :], start=False, stop=True)
                    last.then_inc(out_ready, 1)
                if exists(a):
                    pe.wait_ge(ut_copied, m)
                    if exists(b):
                        pe.wait_ge(state_done, last_t(b))
                    n = steps_of(a) * B
                    rhs = u_t[:, 0:steps_of(a), :]
                    pe.matmul(ps_bu[:, 0, 0:n], bt[:, 0, :], rhs, start=True, stop=True)
                    pe.matmul(ps_bu[:, 1, 0:n], bt[:, 1, :], rhs, start=True, stop=True).then_inc(bu_ready, 1)

            iters = [None]

            def x_iter(m, q):
                return iters[0]

            for q in range(U):
                step(q + 1, q)
            with pe.Fori(1, NQ // U) as i:
                first = i * U
                iters[0] = i * 32
                for q in range(U):
                    step(first + (q + 1), q)
            for m in range(NQ + 1, NQ + 6):
                step(m, (m - 1) % U)

            def split_product(out_ap, stationary, moving, start, stop):
                (wh, wl), (xh, xl) = stationary, moving
                pe.matmul(out_ap, wh, xh, start=start, stop=False)
                pe.matmul(out_ap, wh, xl, start=False, stop=False)
                return pe.matmul(out_ap, wl, xh, start=False, stop=stop)

            def turn(k):
                pe.wait_ge(xn_ready, k + 1)
                wait(pe, xtl_ready, k)
                for j in range(TJ):
                    last = pe.transpose(ps_xt[:, j * 128:(j + 1) * 128], xn[:, j, :], ident)
                last.then_inc(xt_ready, 1)

            def back(k):
                pe.wait_ge(yt_copied, k + 1)
                wait(pe, combined, k)
                for j in range(TJ):
                    last = pe.transpose(ps_y[:, j * 128:(j + 1) * 128], y_t[:, j * 128:(j + 1) * 128], ident)
                last.then_inc(y_ready, 1)

            def tile(k, v, i=None):
                w = w_t[:, WSLOT[v]]
                pe.wait_ge(w_tile_landed[v], (16 if k < V else 16 * (NT // V)) if i is None else i * 16 + 16)
                pe.wait_ge(xtl_ready, k + 1)
                for c in range(FC):
                    wait(pe, gelu_done, k * FC + (c + 1 - FC))
                    split_product(ps_g[c], (w[:, 0, c, :], w[:, 1, c, :]), (xn_t[:, 0, :], xn_t[:, 1, :]),
                                  True, True).then_inc(up_ready, 1)
                if not (isinstance(k, int) and k == NT - 1):
                    turn(k + 1)
                if not (isinstance(k, int) and k == 0):
                    back(k - 1)
                for c in range(FC):
                    pe.wait_ge(low_done, k * FC + (c + 1))
                    last = split_product(ps_yt[:], (w[:, 2, c, :], w[:, 3, c, :]),
                                         (hidden[:, 0, c, :], hidden[:, 1, c, :]), c == 0, c == FC - 1)
                last.then_inc(yt_ready, 1)

            turn(0)
            for_tiles(pe, tile)
            back(NT - 1)

        @block.scalar
        def _(act):
            act.dma_start(vec[:], vecs).then_inc(vec_landed, 16)
            act.dma_start(bri[:], b_ri).then_inc(bc_landed, 16)
            act.dma_start(rhs_s[:, :, 0:HID], c_ph).then_inc(bc_landed, 16)
            act.dma_start(wg_sb[:], wg).then_inc(w_landed, 16)
            act.dma_start(chp[:], c_hp).then_inc(w_landed, 16)
            act.dma_start(wm[:], w_main).then_inc(w_landed, 16)
            act.dma_start(wt[:], w_tail).then_inc(w_landed, 16)
            act.dma_start(pos[:], posT).then_inc(w_landed, 16)
            act.wait_ge(vec_landed, 16)
            act.activation(lam[:, 0:1], vec[:, V_STEP:V_STEP + 1], ACT.Exp).then_inc(setup_act, 1)
            act.wait_ge(setup_act, 1)
            act.activation(lam[:, 1:2], vec[:, V_LR:V_LR + 1], ACT.Exp, scale=lam[:, 0:1]).then_inc(setup_act, 1)
            act.wait_ge(plan_step, 1)
            act.activation(lam[:, 8:10], lam[:, 6:8], ACT.Sin).then_inc(setup_act, 1)
            act.wait_ge(plan_step, 2)
            act.wait_ge(memsets_done, 1)
            act.activation(h_t[:, HSLOT[U - 1], 0, :], zeros[:], ACT.Identity, bias=lam[:, 20:21]).then_inc(h_copied, 1)

            def high_parts(e):
                act.wait_ge(raw_landed[e % 2], 32 * (e // 2 + 1))
                wait(act, w_low, e)
                wait(act, w_stored, 16 * e)
                src = raw[:, e % 2, 0, :].rearrange("d (p c) -> d c p", c=FC)
                gamma = vec[:, V_GAMMA:V_GAMMA + 1]
                act.activation(w1_full[:].rearrange("d (c p) -> d c p", c=FC), src, ACT.Copy, scale=gamma)
                act.activation(split[:, 0, :].rearrange("d (c p) -> d c p", c=FC), src, ACT.Copy, scale=gamma)
                act.activation(split[:, 2, :], raw[:, e % 2, 1, :], ACT.Copy).then_inc(w_high, 1)

            def step(m, q):
                if isinstance(m, int) and m <= E:
                    high_parts(m - 1)
                a, b, d = m - 1, m - 2, m - 4
                if exists(d):
                    n = steps_of(d)
                    act.wait_ge(scaled_ready, m - 3)
                    wait(act, gate_ready, m - 4)
                    act.activation(expd[:, 0:n, :], scaled[:, 0:n, :], ACT.Exp).then_inc(exp_ready, 1)
                if exists(a):
                    act.wait_ge(norm1, m)
                    act.wait_ge(hb_ready, m)
                    wait(act, ut_ready, m - 1)
                    for t in range(steps_of(a)):
                        last = act.activation(u_b[:, t, :], ps_ht[:, t * 128:(t + 1) * 128], ACT.Identity,
                                              bias=nmr1[:, t:t + 1], scale=rs1[:, t:t + 1])
                    last.then_inc(u_ready, 1)
                if exists(m):
                    act.wait_ge(h_summed, m)
                    wait(act, v_ready, m - 1)
                    for t in range(TQ):
                        col = TQ * (m - 1) + (t + 1)
                        bias = pos[:, col:col + 1] if isinstance(m, int) else pos[:, bass.ds(col, 1)]
                        last = act.activation(h_t[:, HSLOT[q], t, :], ps_h[:, t * 128:(t + 1) * 128], ACT.Identity,
                                              bias=bias)
                    last.then_inc(h_copied, 1)
                if exists(a):
                    act.wait_ge(ut_ready, m)
                    wait(act, bu_ready, m - 1)
                    wait(act, v_ready, m - 1)
                    n = steps_of(a)
                    act.activation(u_t[:, 0:n, :], ps_ut[:, 0:n * 128].rearrange("p (t b) -> p t b", t=n), ACT.Copy)\
                        .then_inc(ut_copied, 1)
                if exists(b):
                    act.wait_ge(out_ready, m - 1)
                    qs = slot(q, 2)
                    wait(act, rows_left, m - 7)
                    n = steps_of(b)
                    for g in range((n + 1) // 2):
                        w = min(2, n - 2 * g)
                        last = act.activation(rows[:, qs, 2 * g:2 * g + w, :],
                                              ps_o[g][:, 0:w * ROW].rearrange("p (t c) -> p t c", t=w), ACT.Copy)
                    last.then_inc(row_copied, 1)

            act.wait_ge(setup_dve, 2)
            for q in range(U):
                step(q + 1, q)
            with act.Fori(1, NQ // U) as i:
                first = i * U
                for q in range(U):
                    step(first + (q + 1), q)
            for m in range(NQ + 1, NQ + 6):
                step(m, (m - 1) % U)

            def turned_high(k):
                act.wait_ge(xt_ready, k + 1)
                wait(act, up_ready, k * FC)
                act.activation(xn_t[:, 0, :], ps_xt[:], ACT.Copy).then_inc(xth_ready, 1)

            def copy_y(k):
                act.wait_ge(yt_ready, k + 1)
                wait(act, y_ready, k)
                act.activation(y_t, ps_yt[:], ACT.Copy).then_inc(yt_copied, 1)

            def tile(k, v, i=None):
                if not (isinstance(k, int) and k == 0):
                    copy_y(k - 1)
                for c in range(FC):
                    act.wait_ge(up_ready, k * FC + (c + 1))
                    wait(act, low_done, k * FC + (c + 1 - FC))
                    act.activation(hidden[:, 0, c, :], ps_g[c], ACT.Gelu)
                    act.activation(full[:, c, :], ps_g[c], ACT.Gelu).then_inc(gelu_done, 1)
                if not (isinstance(k, int) and k == NT - 1):
                    turned_high(k + 1)

            turned_high(0)
            for_tiles(act, tile)
            copy_y(NT - 1)

        @block.vector
        def _(dve):
            dve.memset(ones[:], 1.0)
            dve.memset(ones_mean[:], 1.0 / HID)
            dve.memset(eps_t[:], EPS)
            dve.memset(half_t[:], -0.5)
            dve.memset(neg_t[:], -1.0)
            dve.memset(four_t[:], float(TQ))
            dve.memset(one_e[:], 1.0)
            dve.memset(filler[:], 0.0)
            dve.memset(zeros[:], 0.0).then_inc(memsets_done, 1)

            chain = [0]

            def link(ins):
                chain[0] += 1
                ins.then_inc(setup_chain, 1)
                dve.wait_ge(setup_chain, chain[0])

            def col(n):
                return lam[:, n:n + 1]

            def tt(o, x, y, op):
                return dve.tensor_tensor(o, x, y, op)

            dve.wait_ge(memsets_done, 1)
            link(dve.memset(filler[:, :, LISTED - 1:LISTED], NOWHERE))
            dve.wait_ge(setup_act, 1)
            link(tt(col(2), vec[:, V_LI:V_LI + 1], col(0), ALU.mult))
            link(dve.tensor_scalar(col(3), col(2), 0.15915494309189535, 12582912.0, ALU.mult, ALU.add))
            link(dve.tensor_scalar(col(4), col(3), -12582912.0, None, ALU.add))
            link(dve.scalar_tensor_tensor(out=col(5), in0=col(4), scalar=-6.28125, in1=col(2), op0=ALU.mult, op1=ALU.add))
            link(dve.scalar_tensor_tensor(out=col(5), in0=col(4), scalar=-0.0019353071795864769, in1=col(5),
                                          op0=ALU.mult, op1=ALU.add))
            link(dve.tensor_scalar(col(6), col(5), 3.1415925, -3.1415925, ALU.min, ALU.max))
            dve.tensor_scalar(col(7), col(6), 0.5, None, ALU.mult).then_inc(plan_step, 1)
            dve.wait_ge(w_landed, 16 * 5)
            link(tt(col(20), vec[:, V_TOK:V_TOK + 1], pos[:, 0:1], ALU.add))
            dve.tensor_scalar(pos[:, 1:SEQ], pos[:, 1:SEQ], vec[:, V_B:V_B + 1], None, ALU.add).then_inc(plan_step, 1)
            dve.wait_ge(setup_act, 3)
            link(tt(col(10), col(9), col(9), ALU.mult))
            link(dve.tensor_scalar(col(11), col(10), -2.0, 1.0, ALU.mult, ALU.add))
            link(tt(col(12), col(1), col(11), ALU.mult))
            link(tt(col(13), col(1), col(8), ALU.mult))
            link(dve.tensor_scalar(col(14), col(13), -1.0, None, ALU.mult))
            link(dve.tensor_scalar(col(15), col(12), -1.0, None, ALU.add))
            lr, li = vec[:, V_LR:V_LR + 1], vec[:, V_LI:V_LI + 1]
            link(tt(col(16), lr, lr, ALU.mult))
            link(dve.scalar_tensor_tensor(out=col(16), in0=li, scalar=li, in1=col(16), op0=ALU.mult, op1=ALU.add))
            link(dve.reciprocal(col(17), col(16)))
            link(tt(col(18), col(13), li, ALU.mult))
            link(dve.scalar_tensor_tensor(out=col(18), in0=col(15), scalar=lr, in1=col(18), op0=ALU.mult, op1=ALU.add))
            link(tt(col(18), col(18), col(17), ALU.mult))
            link(tt(col(19), col(15), li, ALU.mult))
            link(dve.scalar_tensor_tensor(out=col(19), in0=col(13), scalar=lr, in1=col(19), op0=ALU.mult,
                                          op1=ALU.subtract))
            link(tt(col(19), col(19), col(17), ALU.mult))
            link(dve.tensor_scalar(col(21), col(19), -1.0, None, ALU.mult))
            dve.wait_ge(bc_landed, 32)
            link(dve.tensor_scalar(bbar[:, 0, :], bri[:, 0, :], col(18), None, ALU.mult))
            link(dve.scalar_tensor_tensor(out=bbar[:, 0, :], in0=bri[:, 1, :], scalar=col(21), in1=bbar[:, 0, :],
                                          op0=ALU.mult, op1=ALU.add))
            link(dve.tensor_scalar(bbar[:, 1, :], bri[:, 1, :], col(18), None, ALU.mult))
            link(dve.scalar_tensor_tensor(out=bbar[:, 1, :], in0=bri[:, 0, :], scalar=col(19), in1=bbar[:, 1, :],
                                          op0=ALU.mult, op1=ALU.add))
            dve.wait_ge(setup_pe, 1)
            dve.wait_ge(consts_landed, 16)
            tt(rhs_v[:, HID:ROW], wg_sb[:], ps_h[:, 0:E], ALU.subtract)
            dve.tensor_copy(rhs_v[:, 0:HID], ident)
            dve.tensor_copy(tri[:], cst[:, C_TRI:C_TRI + 128])
            dve.tensor_copy(base[:, 0, :], cst[:, C_BASE:C_BASE + E])
            dve.tensor_scalar(rhs_s[:, 0, 0:HID], rhs_s[:, 0, 0:HID], 2.0, None, ALU.mult)
            dve.tensor_scalar(rhs_s[:, 1, 0:HID], rhs_s[:, 1, 0:HID], -2.0, None, ALU.mult).then_inc(setup_dve, 1)
            dve.wait_ge(setup_pe, 2)
            dve.tensor_copy(bt[:], ps_ht[:, 0:256].rearrange("p (c h) -> p c h", c=2))
            dve.wait_ge(setup_pe, 3)
            dve.tensor_scalar(rhs_s[:, 0, HID:ROW], ps_ut[:, 0:E], 2.0, None, ALU.mult)
            dve.tensor_scalar(rhs_s[:, 1, HID:ROW], ps_ut[:, 64:64 + E], -2.0, None, ALU.mult).then_inc(setup_dve, 1)
            dve.wait_ge(setup_dve, 2)

            re_l, im_l, neg_im_l = col(12), col(13), col(14)
            d_col = vec[:, V_D:V_D + 1]

            def bc_e(x, n):
                return x.rearrange("p (t o) -> p t o", o=1).broadcast_to([128, n, E])

            def step(m, q):
                a, b, c3, c4 = m - 1, m - 2, m - 3, m - 4
                if isinstance(m, int) and m <= E:
                    dve.wait_ge(w_high, m)
                    tt(split[:, 1, :], w1_full[:], split[:, 0, :].bitcast(F32), ALU.subtract)
                    tt(split[:, 3, :], raw[:, (m - 1) % 2, 1, :], split[:, 2, :].bitcast(F32), ALU.subtract)\
                        .then_inc(w_low, 1)
                if exists(a):
                    dve.wait_ge(hb_ready, m)
                    n = steps_of(a)
                    for t in range(n):
                        last = dve.bn_stats(st1[:, t, :], ps_ht[:, t * 128:(t + 1) * 128])
                    last.then_inc(stats1_parts, 1)
                late = []
                if exists(a):
                    wait(dve, norm1, m - 1)
                    dve.wait_ge(stats1_parts, m)
                if exists(c4):
                    n4 = steps_of(c4)
                    qs4 = slot(q, 4)
                    k4 = m - 3
                    dve.wait_ge(rs2_ready, k4)
                    dve.wait_ge(below_ready, k4)
                    tt(scaled[:, 0:n4, :], below[:, 0:n4, :], bc_e(rs2[:, 0, 0:n4], n4), ALU.mult)\
                        .then_inc(scaled_ready, 1)
                if exists(a):
                    for t in range(steps_of(a)):
                        last = dve.bn_aggr(mv1[:, t, :], st1[:, t, :])
                    last.then_inc(moments1, 1)
                if exists(c4):
                    def r_place():
                        dve.wait_ge(rank_ready, k4)
                        wait(dve, base_ready, k4 - 1)
                        tt(place[:, 0:n4, :], ps_rank[:, 0:n4 * E].rearrange("p (t e) -> p t e", e=E),
                           base[:, 0, :].rearrange("p (o e) -> p o e", o=1).broadcast_to([128, n4, E]), ALU.add)\
                            .then_inc(place_ready, 1)

                    def r_base():
                        dve.wait_ge(place_ready, k4)
                        tt(base[:, 0, :], base[:, 0, :], ps_rank[:, TQ * E:(TQ + 1) * E], ALU.add)\
                            .then_inc(base_ready, 1)

                    def r_sum():
                        dve.wait_ge(exp_ready, k4)
                        dve.tensor_reduce(exp_sum[:, 0:n4], expd[:, 0:n4, :], AX, ALU.add).then_inc(sum_ready, 1)

                    def r_others():
                        dve.scalar_tensor_tensor(out=others[:, 0:n4, :], in0=chosen[:, 0:n4, :], scalar=0.0,
                                                 in1=expd[:, 0:n4, :], op0=ALU.is_equal, op1=ALU.mult)\
                            .then_inc(others_ready, 1)

                    def r_at():
                        tt(listed_at[:, 0:n4, :], place[:, 0:n4, :], chosen[:, 0:n4, :], ALU.mult)\
                            .then_inc(at_ready, 1)

                    def r_second():
                        dve.wait_ge(others_ready, k4)
                        dve.tensor_reduce(second[:, 0:n4], others[:, 0:n4, :], AX, ALU.max).then_inc(second_ready, 1)

                    def r_destf():
                        dve.wait_ge(at_ready, k4)
                        dve.tensor_reduce(dest_f[:, 0:n4], listed_at[:, 0:n4, :], AX, ALU.add).then_inc(destf_ready, 1)

                    def r_den():
                        dve.wait_ge(sum_ready, k4)
                        dve.wait_ge(second_ready, k4)
                        dve.scalar_tensor_tensor(out=gate_den[:, 0:n4], in0=exp_sum[:, 0:n4], scalar=GATE_EPS,
                                                 in1=second[:, 0:n4], op0=ALU.mult, op1=ALU.add).then_inc(den_ready, 1)

                    def r_dest():
                        dve.wait_ge(destf_ready, k4)
                        dve.tensor_copy(dest[:, qs4, 0:n4], dest_f[:, 0:n4]).then_inc(dest_ready, 1)

                    def r_den1():
                        dve.wait_ge(den_ready, k4)
                        dve.tensor_scalar(gate_den1[:, 0:n4], gate_den[:, 0:n4], 1.0, None, ALU.add)\
                            .then_inc(den1_ready, 1)

                    def r_gate():
                        dve.wait_ge(den1_ready, k4)
                        dve.reciprocal(rows[:, qs4, 0:n4, HID + 2], gate_den1[:, 0:n4]).then_inc(gate_ready, 1)

                    late = [(r_place, ), (r_base, ), (r_sum, r_at), (r_others, r_destf), (r_second, r_dest), (r_den, ),
                            (r_den1, ), (r_gate, )]

                early = []
                if exists(c3):
                    n3 = steps_of(c3)
                    qs3 = slot(q, 3)
                    k3 = m - 2
                    row3 = rows[:, qs3, 0:n3, :]

                    def s_stats():
                        dve.wait_ge(row_copied, k3)
                        for t in range(n3):
                            last = dve.bn_stats(st2[:, t, :], rows[:, qs3, t, 0:HID])
                        last.then_inc(stats2_parts, 1)

                    def s_top():
                        dve.tensor_reduce(top[:, 0:n3], row3[:, :, RAW:RAW + E], AX, ALU.max).then_inc(top_ready, 1)

                    def s_aggr():
                        for t in range(n3):
                            last = dve.bn_aggr(mv2[:, t, :], st2[:, t, :])
                        last.then_inc(moments2, 1)

                    def s_below():
                        dve.wait_ge(stats2_parts, k3)
                        wait(dve, nmr2_ready, k3 - 1)
                        dve.wait_ge(top_ready, k3)
                        tt(below[:, 0:n3, :], row3[:, :, RAW:RAW + E], bc_e(top[:, 0:n3], n3), ALU.subtract)\
                            .then_inc(below_ready, 1)

                    def s_key():
                        dve.wait_ge(below_ready, k3)
                        dve.scalar_tensor_tensor(out=key[:, 0:n3, :], in0=below[:, 0:n3, :], scalar=0.0,
                                                 in1=tie_weight[:, 0:n3, :], op0=ALU.is_equal, op1=ALU.mult)\
                            .then_inc(key_ready, 1)

                    def s_keytop():
                        dve.wait_ge(key_ready, k3)
                        dve.tensor_reduce(key_top[:, 0:n3], key[:, 0:n3, :], AX, ALU.max).then_inc(keytop_ready, 1)

                    def s_chosen():
                        dve.wait_ge(keytop_ready, k3)
                        tt(chosen[:, 0:n3, :], key[:, 0:n3, :], bc_e(key_top[:, 0:n3], n3), ALU.is_equal)\
                            .then_inc(chosen_ready, 1)

                    early = [s_stats, s_top, s_below, s_aggr]

                if exists(b):
                    dve.wait_ge(bu_ready, m - 1)
                    wait(dve, out_ready, m - 2)
                    if isinstance(b, int) and b == 0:
                        dve.tensor_copy(states[:, TQ - 1, :, :], ps_bu[:, :, 0:B])
                        dve.tensor_copy(states[:, 0, :, :], ps_bu[:, :, 0:B]).then_inc(state_done, 1)
                    else:
                        for t in range(TQ):
                            T = last_t(b) - TQ + t
                            pv = (t - 1) % TQ
                            dd = decayed[:, t % 2, :, :]
                            dve.wait_ge(state_done, T)
                            dve.scalar_tensor_tensor(out=dd, in0=states[:, pv, :, :], scalar=re_l,
                                                     in1=ps_bu[:, :, t * B:(t + 1) * B], op0=ALU.mult, op1=ALU.add)\
                                .then_inc(decay_done, 1)
                            if late:
                                for f in late.pop(0):
                                    f()
                            dve.wait_ge(decay_done, T)
                            dve.scalar_tensor_tensor(out=states[:, t, 0, :], in0=states[:, pv, 1, :], scalar=neg_im_l,
                                                     in1=dd[:, 0, :], op0=ALU.mult, op1=ALU.add)
                            dve.scalar_tensor_tensor(out=states[:, t, 1, :], in0=states[:, pv, 0, :], scalar=im_l,
                                                     in1=dd[:, 1, :], op0=ALU.mult, op1=ALU.add)\
                                .then_inc(state_done, 1)
                            if late:
                                for f in late.pop(0):
                                    f()
                for fs in late:
                    for f in fs:
                        f()
                for f in early:
                    f()
                if exists(a):
                    n = steps_of(a)
                    sv = HSLOT[slot(q, 1)]
                    dve.wait_ge(ut_copied, m)
                    wait(dve, out_ready, m - 2)
                    if exists(c3):
                        s_key()
                    dve.scalar_tensor_tensor(out=v_t[:, sv, 0:n, :], in0=u_t[:, 0:n, :], scalar=d_col,
                                             in1=h_t[:, sv, 0:n, :], op0=ALU.mult, op1=ALU.add).then_inc(v_ready, 1)
                elif exists(c3):
                    s_key()
                if exists(c3):
                    s_keytop()
                    s_chosen()

            for_steps(dve, step)

            pchain = [2]

            def plink(ins):
                pchain[0] += 1
                ins.then_inc(plan_step, 1)
                dve.wait_ge(plan_step, pchain[0])

            dve.wait_ge(base_ready, NQ + 1)
            cst0 = cst[0:1, :]
            plink(tt(count[:], base[0:1, 0, :], cst0[:, C_BASE:C_BASE + E], ALU.subtract))
            plink(tt(cmp_t[:], count[:].rearrange("o (e j) -> o e j", j=1).broadcast_to([1, E, MAXT]),
                     cst0[:, C_GRID:C_GRID + MAXT].rearrange("o (e j) -> o e j", e=1).broadcast_to([1, E, MAXT]),
                     ALU.is_gt))
            plink(dve.tensor_reduce(ntile[:], cmp_t[:], AX, ALU.add))
            plink(dve.tensor_tensor_scan(cum[:], one_e[:], ntile[:], 0.0, ALU.mult, ALU.add))
            grid_k = cst0[:, C_K:C_K + NT]
            plink(tt(passed[:], grid_k.rearrange("o (k e) -> o k e", e=1).broadcast_to([1, NT, E]),
                     cum[:].rearrange("o (k e) -> o k e", k=1).broadcast_to([1, NT, E]), ALU.is_ge))
            plink(dve.tensor_reduce(expert_f[:], passed[:], AX, ALU.add))
            plink(tt(before[:], passed[:], ntile[:].rearrange("o (k e) -> o k e", k=1).broadcast_to([1, NT, E]),
                     ALU.mult))
            plink(dve.tensor_reduce(before_f[:], before[:], AX, ALU.add))
            plink(tt(start_f[:, 0, :], grid_k, before_f[:], ALU.subtract))
            plink(dve.tensor_scalar(start_f[:, 1, :], expert_f[:], float(REGION), None, ALU.mult))
            plink(dve.scalar_tensor_tensor(out=start_f[:, 2, :], in0=start_f[:, 0, :], scalar=float(TILE),
                                           in1=start_f[:, 1, :], op0=ALU.mult, op1=ALU.add))
            plink(dve.tensor_scalar(start_i[:], start_f[:, 2, :], float(E * REGION), None, ALU.min))
            plink(dve.tensor_scalar(weights_f[:], expert_f[:], float(HID), None, ALU.mult))
            plink(dve.tensor_scalar(weights_i[:], weights_f[:], float((E - 1) * HID), None, ALU.min))
            dve.tensor_copy(base_i[:], base[0:1, 0, :]).then_inc(plan_ready, 1)
            def normalise(k, v, landed):
                dve.wait_ge(tile_landed[v], landed)
                wait(dve, xt_ready, k)
                for j in range(TJ):
                    last = dve.tensor_scalar(xn[:, j, :], lt[:, v, j, 0:HID], lt[:, v, j, HID:HID + 1],
                                             lt[:, v, j, HID + 1:HID + 2], ALU.mult, ALU.add)
                last.then_inc(xn_ready, 1)

            def turned_low(k):
                dve.wait_ge(xth_ready, k + 1)
                dve.tensor_tensor(xn_t[:, 1, :], ps_xt[:], xn_t[:, 0, :].bitcast(F32), ALU.subtract)\
                    .then_inc(xtl_ready, 1)

            def combine(k, v):
                wait(dve, results_left, k - 3)
                dve.tensor_copy(place_i[:, v, :], lt[:, v, :, HID + 3]).then_inc(placei_ready, 1)
                dve.wait_ge(y_ready, k + 1)
                for j in range(TJ):
                    last = dve.scalar_tensor_tensor(out=res[:, v, j, :], in0=ps_y[:, j * 128:(j + 1) * 128],
                                                    scalar=lt[:, v, j, HID + 2:HID + 3], in1=lt[:, v, j, 0:HID],
                                                    op0=ALU.mult, op1=ALU.add)
                last.then_inc(combined, 1)

            def tile(k, v, i=None):
                for c in range(FC):
                    dve.wait_ge(gelu_done, k * FC + (c + 1))
                    if c == 0:
                        wait(dve, yt_ready, k)
                    dve.tensor_tensor(hidden[:, 1, c, :], full[:, c, :], hidden[:, 0, c, :].bitcast(F32),
                                      ALU.subtract).then_inc(low_done, 1)
                if not (isinstance(k, int) and k == 0):
                    combine(k - 1, (v - 1) % V)
                if not (isinstance(k, int) and k == NT - 1):
                    turned_low(k + 1)
                if not (isinstance(k, int) and k >= NT - 2):
                    nv = (v + 2) % V
                    if i is None:
                        landed = 16 * ((k + 2) // V + 1)
                    else:
                        landed = i * 16 + (16 if v + 2 < V else 32)
                    normalise(k + 2, nv, landed)

            normalise(0, 0, 16)
            turned_low(0)
            normalise(1, 1, 16)
            for_tiles(dve, tile)
            combine(NT - 1, V - 1)

        @block.gpsimd
        def _(pool):
            def tt(o, x, y, op):
                return pool.tensor_tensor(o, x, y, op)

            pool.wait_ge(memsets_done, 1)
            pool.wait_ge(vec_landed, 16)
            pool.tensor_copy(out_row[:, 0:1], vec[:, V_IMG:V_IMG + 1]).then_inc(outrow_ready, 1)

            def step(m, q):
                a, c3, c5 = m - 1, m - 3, m - 5
                if exists(a):
                    n = steps_of(a)
                    pool.wait_ge(moments1, m)
                    wait(pool, u_ready, m - 1)
                    tt(ve1[:, 0:n], mv1[:, 0:n, 1], eps_t[:, 0:n], ALU.add).then_inc(ve1_ready, 1)
                    tt(nm1[:, 0:n], mv1[:, 0:n, 0], neg_t[:, 0:n], ALU.mult).then_inc(nm1_ready, 1)
                    pool.wait_ge(ve1_ready, m)
                    tt(rs1[:, 0:n], ve1[:, 0:n], half_t[:, 0, 0:n], ALU.pow).then_inc(rs1_ready, 1)
                    pool.wait_ge(rs1_ready, m)
                    pool.wait_ge(nm1_ready, m)
                    tt(nmr1[:, 0:n], nm1[:, 0:n], rs1[:, 0:n], ALU.mult).then_inc(norm1, 1)
                j = m - 6
                if exists(j):
                    qs = slot(q, 6)
                    own = 16 if qs == U - 1 else 0
                    if isinstance(m, int):
                        pool.wait_ge(listed[qs], 16 * TQ * ((j - 1) // U + 1) + own)
                    else:
                        pool.wait_ge(listed[qs], iters[0] + ((16 * TQ if q == U - 1 else 0) + own))
                    pool.sem_inc(rows_left, 1)
                if exists(c5):
                    n = steps_of(c5)
                    qs = slot(q, 5)
                    pool.wait_ge(gate_ready, m - 4)
                    pool.wait_ge(dest_ready, m - 4)
                    pool.wait_ge(meta_ready, m - 4)
                    pool.sem_inc(pool_passed, 1)
                    for t in range(n):
                        pool.indirect_dma_start(
                            out=lists, out_offset=bass.IndirectOffsetOnAxis(ap=dest[:, qs, t:t + 1], axis=0),
                            in_=rows[:, qs, t, 0:LISTED], in_offset=None,
                            bounds_check=E * REGION - 1, oob_is_err=True).then_inc(listed[qs], 16)
                if exists(c3):
                    n = steps_of(c3)
                    qs = slot(q, 3)
                    k = m - 2
                    pool.wait_ge(moments2, k)
                    wait(pool, scaled_ready, k - 1)
                    tt(ve2[:, 0, 0:n], mv2[:, 0:n, 1], eps_t[:, 0:n], ALU.add).then_inc(ve2a_ready, 1)
                    tt(nm2[:, 0:n], mv2[:, 0:n, 0], neg_t[:, 0:n], ALU.mult).then_inc(nm2_ready, 1)
                    pool.wait_ge(ve2a_ready, k)
                    tt(ve2[:, 1, 0:n], ve2[:, 0, 0:n], eps_t[:, 0:n], ALU.mult).then_inc(ve2b_ready, 1)
                    pool.wait_ge(ve2b_ready, k)
                    tt(ve2[:, 1, 0:n], ve2[:, 1, 0:n], mv2[:, 0:n, 1], ALU.add).then_inc(ve2c_ready, 1)
                    pool.wait_ge(ve2c_ready, k)
                    tt(rs2[:, :, 0:n], ve2[:, :, 0:n], half_t[:, :, 0:n], ALU.pow).then_inc(rs2_ready, 1)
                    pool.wait_ge(rs2_ready, k)
                    pool.wait_ge(below_ready, k)
                    pool.wait_ge(nm2_ready, k)
                    tt(rows[:, qs, 0:n, HID + 1], nm2[:, 0:n], rs2[:, 1, 0:n], ALU.mult).then_inc(nmr2_ready, 1)
                    pool.tensor_copy(rows[:, qs, 0:n, HID], rs2[:, 1, 0:n])
                    pool.wait_ge(outrow_ready, k)
                    pool.sem_inc(pool_passed, 1)
                    pool.tensor_copy(rows[:, qs, 0:n, HID + 3], out_row[:, 0:n]).then_inc(meta_ready, 1)
                    pool.wait_ge(meta_ready, k)
                    if isinstance(m, int) and c3 == 0:
                        for t in range(TQ):
                            last = pool.tensor_scalar(out_row[:, t:t + 1], vec[:, V_IMG:V_IMG + 1], float(t + 1), None,
                                                      ALU.add)
                        last.then_inc(outrow_ready, 1)
                    else:
                        tt(out_row[:], out_row[:], four_t[:], ALU.add).then_inc(outrow_ready, 1)

            iters = [None]
            for q in range(U):
                step(q + 1, q)
            with pool.Fori(1, NQ // U) as i:
                first = i * U
                iters[0] = i * (16 * TQ)
                for q in range(U):
                    step(first + (q + 1), q)
            for m in range(NQ + 1, NQ + 6):
                step(m, (m - 1) % U)

            def store_tile(k, v, i=0):
                pool.wait_ge(placei_ready, k + 1)
                pool.wait_ge(combined, k + 1)
                pool.sem_inc(pool_passed, 1)
                for j in range(TJ):
                    pool.indirect_dma_start(
                        out=out, out_offset=bass.IndirectOffsetOnAxis(ap=place_i[:, v, j:j + 1], axis=0),
                        in_=res[:, v, j, :], in_offset=None,
                        bounds_check=NTOK - 1, oob_is_err=False).then_inc(stored[v], 16)
                if not (isinstance(k, int) and k < 2):
                    pool.wait_ge(stored[(v - 2) % V], 16 * TJ * ((k - 2) // V + 1) if isinstance(k, int) else
                                 i * (16 * TJ) + (16 * TJ if v >= 2 else 0))
                    pool.sem_inc(results_left, 1)

            for_tiles(pool, store_tile)


def kernel(**inputs):
    import numpy as np
    import concourse.bacc as bacc
    from concourse.bass_utils import run_bass_kernel_spmd

    get = {k: np.asarray(v) for k, v in inputs.items()}
    x = get["x"].reshape(B, 3, GRID, 14, GRID, 14).transpose(2, 4, 1, 3, 5, 0).reshape(NQ, TQ, IN_DIM, B)
    x = x.transpose(0, 2, 1, 3)
    w = get["L0_tok_W"].T
    bm, cm = get["L0_attn_B"], get["L0_attn_C"]
    images = np.arange(B, dtype=np.float32) * SEQ
    consts = np.zeros((128, C_END), np.float32)
    consts[:, C_ID:C_ID + 128] = np.eye(128)
    consts[:, C_TRI:C_TRI + 128] = np.triu(np.ones((128, 128)), 1)
    consts[:, C_WT:C_WT + TQ * E] = np.tile(np.arange(E, 0, -1), TQ)
    consts[:, C_BASE:C_BASE + E] = np.arange(E) * REGION
    consts[:, C_GRID:C_GRID + MAXT] = np.arange(MAXT) * TILE
    consts[:, C_K:C_K + NT] = np.arange(NT)
    arrays = {
        "x_main": x[:, :KC * 128].reshape(NQ, KC, 128, TQ * B).transpose(0, 2, 1, 3),
        "x_tail": x[:, KC * 128:].reshape(NQ, KT, TQ * B),
        "w_main": w[:KC * 128].reshape(KC, 128, HID).transpose(1, 0, 2),
        "w_tail": w[KC * 128:],
        "vecs": np.stack([get["L0_attn_lambda_real"], get["L0_attn_lambda_imag"], get["L0_attn_log_step"][:, 0],
                          get["L0_attn_D"], get["L0_tok_b"], get["L0_tok_token"][0], get["L0_ffn_gamma"], images], 1),
        "posT": get["L0_tok_pos"].T,
        "b_ri": bm.transpose(0, 2, 1),
        "c_hp": cm.transpose(0, 2, 1),
        "c_ph": cm.transpose(1, 2, 0),
        "wg": get["L0_ffn_w_gating"],
        "w1": get["L0_ffn_w1"],
        "w2": get["L0_ffn_w2"],
        "consts": consts,
    }
    nc = bacc.Bacc("TRN2", target_bir_lowering=False, num_devices=1)
    args = []
    for name in arrays:
        a = arrays[name] = np.ascontiguousarray(arrays[name])
        args.append(nc.dram_tensor(name, a.shape, mybir.dt.from_np(a.dtype), kind="ExternalInput").ap())
    args.append(nc.dram_tensor("out", (NTOK, HID), F32, kind="ExternalOutput").ap())
    build(nc, *args)
    r = run_bass_kernel_spmd(nc, [arrays], core_ids=[0])
    return r.results[0]["out"].reshape(B, SEQ, HID)
```

```python
from contextlib import ExitStack

import concourse.bass as bass
from concourse import mybir

ALU = mybir.AluOpType
ACT = mybir.ActivationFunctionType
AX = mybir.AxisListType.X
F32 = mybir.dt.float32
F32R = mybir.dt.float32r
BF16 = mybir.dt.bfloat16
I32 = mybir.dt.int32
U32 = mybir.dt.uint32

B = 128
HID = 128
GRID = 14
IN_DIM = 3 * 14 * 14
SEQ = GRID * GRID + 1
KC = IN_DIM // 128
KT = IN_DIM - KC * 128
TQ = 4
NQ = (SEQ - 1) // TQ
U = 7
XB = 4
E = 6
FF = 512
FC = FF // 128
EPS = 1e-5
GATE_EPS = 1e-9
CAPACITY = max(min(SEQ, int(SEQ * 6.0 / E)), 4)
assert CAPACITY == SEQ and NQ % U == 0

NTOK = B * SEQ
TILE = 512
TJ = TILE // 128
REGION = NTOK + TILE
NT = (NTOK + E * (TILE - 1)) // TILE
V = 5
NT += -NT % V
LISTED = 132
RAW = HID
ROW = HID + E
NOWHERE = float(NTOK + 1000)
MAXT = (NTOK + TILE - 1) // TILE

V_LR, V_LI, V_STEP, V_D, V_B, V_TOK, V_GAMMA, V_IMG = range(8)
C_ID, C_TRI, C_WT = 0, 128, 256
C_BASE = C_WT + TQ * E
C_GRID = C_BASE + E
C_K = C_GRID + MAXT
C_END = C_K + NT


def build(nc, x_main, x_tail, w_main, w_tail, vecs, posT, b_ri, c_hp, c_ph, wg, w1, w2, consts, out):
    with ExitStack() as ctx:
        def sb(name, shape, dt=F32):
            return ctx.enter_context(nc.sbuf_tensor(name, shape, dt))

        def sem(name):
            return ctx.enter_context(nc.semaphore(name))

        def psum(name, *shape):
            return ctx.enter_context(nc.psum_tensor(name, [128, *shape], F32))

        ps_h, ps_ht, ps_ut, ps_bu = psum("ps_h", 512), psum("ps_ht", 512), psum("ps_ut", 512), psum("ps_bu", 2, 512)
        ps_o = [psum("ps_o0", 512), psum("ps_o1", 512)]
        ps_rank = psum("ps_rank", 512)
        ps_g = [ps_ht[:], ps_ut[:], ps_bu[:, 0, :], ps_bu[:, 1, :]]
        ps_xt = ps_y = ps_h
        ps_yt = [*ps_o, ps_rank]

        lists = nc.dram_tensor("lists", [E * REGION + TILE, LISTED], F32).ap()
        cst = sb("cst", [128, C_END])
        ident = cst[:, C_ID:C_ID + 128]
        tie_weight = cst[:, C_WT:C_WT + TQ * E].rearrange("p (t e) -> p t e", e=E)
        vec = sb("vec", [128, 8])
        pos = sb("pos", [128, SEQ])
        wm = sb("wm", [128, KC, HID])
        wt = sb("wt", [KT, HID])
        bri = sb("bri", [128, 2, HID])
        chp = sb("chp", [128, 2, HID])
        wg_sb = sb("wg_sb", [128, E])
        lam = sb("lam", [128, 24])
        warm = sb("warm", [128, 1])
        bbar = sb("bbar", [128, 2, HID])
        bt = sb("bt", [128, 2, 2, HID], F32R)
        rhs_v = sb("rhs_v", [128, ROW])
        rhs_s = sb("rhs_s", [128, 2, ROW])
        tri = sb("tri", [128, 128], BF16)
        ones = sb("ones", [128, 128], BF16)
        ones_mean = sb("ones_mean", [128, 128])
        zeros = sb("zeros", [128, 128])
        eps_t = sb("eps_t", [128, TQ])
        half_t = sb("half_t", [128, 2, TQ])
        neg_t = sb("neg_t", [128, TQ])
        four_t = sb("four_t", [128, TQ])
        xm = sb("xm", [128, XB, KC, TQ * B])
        xt = sb("xt", [KT, XB, TQ * B])
        h_t = sb("h_t", [128, 3, TQ, B])
        u_b = sb("u_b", [128, TQ, HID])
        u_t = sb("u_t", [128, 2, TQ * B], F32R)
        v_t = sb("v_t", [128, 3, TQ, B])
        states = sb("states", [128, TQ, 2, B])
        decayed = sb("decayed", [128, 2, 2, B])
        st1 = sb("st1", [128, TQ, 6])
        mv1 = sb("mv1", [128, TQ, 2])
        ve1 = sb("ve1", [128, TQ])
        rs1 = sb("rs1", [128, TQ])
        nm1 = sb("nm1", [128, TQ])
        nmr1 = sb("nmr1", [128, TQ])
        rows = sb("rows", [128, U, TQ, ROW])
        st2 = sb("st2", [128, TQ, 6])
        mv2 = sb("mv2", [128, TQ, 2])
        ve2 = sb("ve2", [128, 2, TQ])
        rs2 = sb("rs2", [128, 2, TQ])
        nm2 = sb("nm2", [128, TQ])
        out_row = sb("out_row", [128, TQ])
        top = sb("top", [128, TQ])
        below = sb("below", [128, TQ, E])
        key = sb("key", [128, TQ, E])
        key_top = sb("key_top", [128, TQ])
        chosen = sb("chosen", [128, TQ + 1, E], BF16)
        scaled = sb("scaled", [128, TQ, E])
        expd = sb("expd", [128, TQ, E])
        exp_sum = sb("exp_sum", [128, TQ])
        others = sb("others", [128, TQ, E])
        second = sb("second", [128, TQ])
        gate_den = sb("gate_den", [128, TQ])
        gate_den1 = sb("gate_den1", [128, TQ])
        place = sb("place", [128, TQ, E])
        listed_at = sb("listed_at", [128, TQ, E])
        dest_f = sb("dest_f", [128, TQ])
        dest = sb("dest", [128, U, TQ], U32)
        base = sb("base", [128, 2, E])
        filler = sb("filler", [128, TJ, LISTED])
        count = sb("count", [1, E])
        cmp_t = sb("cmp_t", [1, E, MAXT])
        ntile = sb("ntile", [1, E])
        one_e = sb("one_e", [1, E])
        cum = sb("cum", [1, E])
        passed = sb("passed", [1, NT, E])
        expert_f = sb("expert_f", [1, NT])
        before = sb("before", [1, NT, E])
        before_f = sb("before_f", [1, NT])
        start_f = sb("start_f", [1, 3, NT])
        start_i = sb("start_i", [1, NT], I32)
        weights_f = sb("weights_f", [1, NT])
        weights_i = sb("weights_i", [1, NT], I32)
        base_i = sb("base_i", [1, E], I32)
        w1_full = sb("w1_full", [128, 2, FF])
        w_all = sb("w_all", [128, E, 4, FF], F32R)
        patches = xm[:].rearrange("p u c n -> p (u c n)")
        used = [0]

        def in_patches(n, pattern, **sizes):
            used[0] += n
            assert used[0] <= XB * KC * TQ * B
            return patches[:, used[0] - n:used[0]].rearrange(pattern, **sizes)

        raw = in_patches(2 * E * FF, "p (l e f) -> p l e f", l=2, e=E)
        used[0] = 0
        lt = in_patches(V * TJ * LISTED, "p (v j c) -> p v j c", v=V, j=TJ)
        xn = in_patches(TJ * HID, "p (j c) -> p j c", j=TJ)
        full = in_patches(FC * TILE, "p (c s) -> p c s", c=FC)
        y_t = u_b[:].rearrange("p t b -> p (t b)")
        res = in_patches(V * TJ * HID, "p (v j c) -> p v j c", v=V, j=TJ)
        w_t = sb("w_t", [128, 3, 4, FC, 128], F32R)
        xn_t = sb("xn_t", [128, 2, TILE], F32R)
        hidden = sb("hidden", [128, 2, FC, TILE], F32R)
        place_i = sb("place_i", [128, V, TJ], U32)

        consts_landed, vec_landed, w_landed = sem("consts_landed"), sem("vec_landed"), sem("w_landed")
        bc_landed = sem("bc_landed")
        pool_passed = sem("pool_passed")
        memsets_done, setup_dve, setup_act, setup_pe, setup_chain = (
            sem("memsets_done"), sem("setup_dve"), sem("setup_act"), sem("setup_pe"), sem("setup_chain"))
        angles_ready, pos_ready = sem("angles_ready"), sem("pos_ready")
        x_landed = [sem(f"x_landed{q}") for q in range(U)]
        h_summed, h_copied = sem("h_summed"), sem("h_copied")
        hb_ready, moments1, stats1_parts = sem("hb_ready"), sem("moments1"), sem("stats1_parts")
        ve1_ready, nm1_ready, rs1_ready, norm1 = sem("ve1_ready"), sem("nm1_ready"), sem("rs1_ready"), sem("norm1")
        u_ready, ut_ready, v_ready = sem("u_ready"), sem("ut_ready"), sem("v_ready")
        ut_high, ut_low = sem("ut_high"), sem("ut_low")
        bu_ready = sem("bu_ready")
        decay_done, state_done = sem("decay_done"), sem("state_done")
        out_ready, row_copied = sem("out_ready"), sem("row_copied")
        stats2_parts, moments2 = sem("stats2_parts"), sem("moments2")
        ve2a_ready, ve2b_ready, ve2c_ready = sem("ve2a_ready"), sem("ve2b_ready"), sem("ve2c_ready")
        rs2_ready, nm2_ready, nmr2_ready = sem("rs2_ready"), sem("nm2_ready"), sem("nmr2_ready")
        outrow_ready, meta_ready = sem("outrow_ready"), sem("meta_ready")
        top_ready, below_ready, key_ready, keytop_ready, chosen_ready = (
            sem("top_ready"), sem("below_ready"), sem("key_ready"), sem("keytop_ready"), sem("chosen_ready"))
        scaled_ready, exp_ready, sum_ready, others_ready, second_ready = (
            sem("scaled_ready"), sem("exp_ready"), sem("sum_ready"), sem("others_ready"), sem("second_ready"))
        den_ready, den1_ready, gate_ready = sem("den_ready"), sem("den1_ready"), sem("gate_ready")
        rank_ready, place_ready, base_ready, at_ready, destf_ready, dest_ready = (
            sem("rank_ready"), sem("place_ready"), sem("base_ready"), sem("at_ready"), sem("destf_ready"),
            sem("dest_ready"))
        listed = [sem(f"listed{q}") for q in range(U)]
        rows_left = sem("rows_left")
        plan_step, plan_ready, filled = sem("plan_step"), sem("plan_ready"), sem("filled")
        raw_landed = sem("raw_landed")
        w_high, w_low = sem("w_high"), sem("w_low")
        tile_landed = [sem(f"tile_landed{v}") for v in range(V)]
        w_tile_landed = [sem(f"w_tile_landed{v}") for v in range(V)]
        xn_ready, xt_ready, xth_ready, xtl_ready = sem("xn_ready"), sem("xt_ready"), sem("xth_ready"), sem("xtl_ready")
        up_ready, high_done, gelu_done, low_done, down_done = (
            sem("up_ready"), sem("high_done"), sem("gelu_done"), sem("low_done"), sem("down_done"))
        yt_copied, y_ready, combined, placei_ready = (
            sem("yt_copied"), sem("y_ready"), sem("combined"), sem("placei_ready"))
        stored = [sem(f"stored{v}") for v in range(V)]
        results_left = sem("results_left")

        block = ctx.enter_context(nc.Block())

        def wait(eng, s, value):
            if not (isinstance(value, int) and value <= 0):
                eng.wait_ge(s, value)

        def exists(m):
            return not isinstance(m, int) or 0 <= m <= NQ

        def steps_of(m):
            return 1 if isinstance(m, int) and m == 0 else TQ

        def last_t(m):
            return TQ * m + 1

        HSLOT = [0, 1, 0, 1, 0, 1, 2]
        XSLOT = [0, 1, 2, 0, 1, 2, 3]
        SLOT3 = [0, 1, 0, 1, 2]

        def for_tiles(eng, step):
            for v in range(V):
                step(v, v)
            with eng.Fori(1, NT // V - 1) as i:
                first = i * V
                for v in range(V):
                    step(first + v, v, i)
            for v in range(V):
                step(NT - V + v, v)

        def for_steps(eng, step):
            for q in range(U):
                step(q + 1, q)
            with eng.Fori(1, NQ // U) as i:
                first = i * U
                for q in range(U):
                    step(first + (q + 1), q)
            for m in range(NQ + 1, NQ + 6):
                step(m, (m - 1) % U)

        def slot(q, lag):
            return (q - lag) % U

        @block.sync
        def _(sp):
            def load(m, q):
                wait(sp, h_summed, m - 3)
                ix = m - 1
                sp.dma_start(xm[:, XSLOT[q], :, :], x_main[ix] if isinstance(m, int) else
                             x_main[bass.ds(ix, 1)].rearrange("o p c n -> (o p) c n")).then_inc(x_landed[q], 16)
                sp.dma_start(xt[:, XSLOT[q], :], x_tail[ix] if isinstance(m, int) else
                             x_tail[bass.ds(ix, 1)].rearrange("o p n -> (o p) n")).then_inc(x_landed[q], 16)

            sp.dma_start(wg_sb[:], wg).then_inc(w_landed, 16)
            sp.dma_start(wm[:], w_main).then_inc(w_landed, 16)
            sp.dma_start(wt[:], w_tail).then_inc(w_landed, 16)
            load(1, 0)
            sp.dma_start(chp[:], c_hp).then_inc(w_landed, 16)
            sp.dma_start(cst[:], consts).then_inc(consts_landed, 16)
            for q in range(1, U):
                load(q + 1, q)
            with sp.Fori(1, NQ // U) as i:
                first = sp.snap(i * U)
                for q in range(U):
                    load(first + (q + 1), q)

            sp.wait_ge(h_summed, NQ)
            sp.dma_start(raw[:, 0], w1.rearrange("e d f -> d e f")).then_inc(raw_landed, 16)
            sp.dma_start(raw[:, 1], w2.rearrange("e (p c) d -> p e (c d)", c=FC)).then_inc(raw_landed, 16)

            def at(k):
                return slice(k, k + 1) if isinstance(k, int) else bass.ds(k, 1)

            def weights_of(k):
                start = sp.value_load(weights_i[0:1, at(k)], min_val=0, max_val=(E - 1) * 4 * FF)
                return w_all[:].rearrange("p e s f -> p (e s f)").bitcast(F32)[:, bass.ds(start, 4 * FF)]

            def load_weights(v, w_from):
                sp.dma_start(w_t[:, SLOT3[v]].rearrange("p s c f -> p (s c f)").bitcast(F32), w_from)\
                    .then_inc(w_tile_landed[v], 16)

            def rows_of(k):
                return lists[bass.ds(sp.value_load(start_i[0:1, at(k)], min_val=0, max_val=E * REGION), TILE), :]

            def load_rows(v, rows_from):
                sp.dma_start(lt[:, v, :, :], rows_from.rearrange("(j p) c -> p j c", p=128))\
                    .then_inc(tile_landed[v], 16)

            sp.wait_ge(plan_ready, 1)
            for e in range(E):
                end = sp.value_load(base_i[0:1, e:e + 1], min_val=e * REGION, max_val=e * REGION + NTOK)
                sp.dma_start(lists[bass.ds(end, TILE), :].rearrange("(j p) c -> p j c", p=128), filler[:])\
                    .then_inc(filled, 16)
            sp.dma_start(lists[E * REGION:E * REGION + TILE, :].rearrange("(j p) c -> p j c", p=128), filler[:])\
                .then_inc(filled, 16)
            sp.wait_ge(w_low, E)
            load_weights(0, weights_of(0))
            sp.wait_ge(filled, 16 * (E + 1))
            for q in range(U):
                sp.wait_ge(listed[q], 16 * TQ * (NQ // U) + (16 if q == U - 1 else 0))
            for k in range(2):
                load_rows(k, rows_of(k))
            load_weights(1, weights_of(1))

            def load_tile(k, v, i=0):
                if not (isinstance(k, int) and k < 2):
                    w_from = weights_of(k)
                if not (isinstance(k, int) and k >= NT - 2):
                    rows_from = rows_of(k + 2)
                if not (isinstance(k, int) and k < 2):
                    sp.wait_ge(down_done, (k - 1) * FC)
                    load_weights(v, w_from)
                if not (isinstance(k, int) and k >= NT - 2):
                    wait(sp, combined, k + (3 - V))
                    load_rows((v + 2) % V, rows_from)

            for_tiles(sp, load_tile)
            for v in range(V):
                sp.wait_ge(stored[v], 16 * TJ * (NT // V))

        @block.tensor
        def _(pe):
            pe.wait_ge(w_landed, 16 * 5)
            pe.wait_ge(memsets_done, 1)
            pe.matmul(ps_rank[:, 0:E], ones_mean[:], wg_sb[:], start=True, stop=True).then_inc(setup_pe, 1)
            pe.wait_ge(consts_landed, 16)

            def setup_operands():
                pe.wait_ge(setup_dve, 1)
                for c in range(2):
                    last = pe.transpose(ps_o[0][:, c * 128:(c + 1) * 128], bbar[:, c, :], ident)
                last.then_inc(setup_pe, 1)
                for c in range(2):
                    last = pe.matmul(ps_o[1][:, c * 64:c * 64 + E], chp[:, c, :], rhs_v[:, HID:ROW],
                                     start=True, stop=True)
                last.then_inc(setup_pe, 1)

            def outputs(m, q, ts):
                b = m - 2
                n = steps_of(b)
                sv = HSLOT[slot(q, 2)]
                if 0 in ts:
                    pe.wait_ge(v_ready, m - 1)
                    wait(pe, row_copied, m - 2)
                for t in ts:
                    pe.wait_ge(state_done, last_t(b) - (n - 1 - t))
                    o = ps_o[t // 2][:, (t % 2) * ROW:(t % 2 + 1) * ROW]
                    pe.matmul(o, v_t[:, sv, t, :], rhs_v[:], start=True, stop=False)
                    pe.matmul(o, states[:, t, 0, :], rhs_s[:, 0, :], start=False, stop=False)
                    last = pe.matmul(o, states[:, t, 1, :], rhs_s[:, 1, :], start=False, stop=True)
                    if t == n - 1:
                        last.then_inc(out_ready, 1)

            def ranks(m):
                d = m - 4
                pe.wait_ge(chosen_ready, m - 3)
                wait(pe, base_ready, m - 4)
                n = steps_of(d)
                if n == TQ:
                    pe.matmul(ps_rank[:, 0:(TQ + 1) * E], tri[:], chosen[:].rearrange("p t e -> p (t e)"),
                              start=True, stop=False, skip_group_check=True)
                    for s in range(TQ):
                        last = pe.matmul(
                            ps_rank[:, (s + 1) * E:(TQ + 1) * E].rearrange("p (t e) -> p t e", e=E), ones[:],
                            chosen[:, s:s + 1, :].broadcast_to([128, TQ - s, E]),
                            start=False, stop=(s == TQ - 1), skip_group_check=True)
                else:
                    pe.matmul(ps_rank[:, 0:E], tri[:], chosen[:, 0, :], start=True, stop=True)
                    last = pe.matmul(ps_rank[:, TQ * E:(TQ + 1) * E], ones[:], chosen[:, 0, :],
                                     start=True, stop=True)
                last.then_inc(rank_ready, 1)

            def step(m, q):
                a, b = m - 1, m - 2
                if exists(a):
                    pe.wait_ge(h_copied, m)
                    wait(pe, u_ready, m - 1)
                    for t in range(steps_of(a)):
                        last = pe.transpose(ps_ht[:, t * 128:(t + 1) * 128], h_t[:, HSLOT[slot(q, 1)], t, :], ident)
                    last.then_inc(hb_ready, 1)
                if exists(m):
                    pe.wait_ge(x_landed[q], 32 if isinstance(m, int) else iters[0] + 32)
                    for c in range(KC):
                        pe.matmul(ps_h[:], wm[:, c, :], xm[:, XSLOT[q], c, :], start=(c == 0), stop=False)
                        if c == 0 and exists(m - 4):
                            ranks(m)
                    pe.matmul(ps_h[:], wt[:], xt[:, XSLOT[q], :], start=False, stop=True).then_inc(h_summed, 1)
                elif exists(m - 4):
                    ranks(m)
                if isinstance(m, int) and m == 1:
                    setup_operands()
                if exists(b):
                    outputs(m, q, range(min(2, steps_of(b))))
                if exists(a):
                    pe.wait_ge(u_ready, m)
                    wait(pe, v_ready, m - 1)
                    for t in range(steps_of(a)):
                        last = pe.transpose(ps_ut[:, t * 128:(t + 1) * 128], u_b[:, t, :], ident)
                    last.then_inc(ut_ready, 1)
                if exists(b):
                    outputs(m, q, range(2, steps_of(b)))
                if exists(a):
                    pe.wait_ge(ut_high, m)
                    if isinstance(m, int) and m == 1:
                        pe.wait_ge(setup_dve, 2)
                    if exists(b):
                        pe.wait_ge(state_done, last_t(b))
                    n = steps_of(a) * B
                    for part in range(2):
                        for c in range(2):
                            pe.matmul(ps_bu[:, c, 0:n], bt[:, part, c, :], u_t[:, 0, 0:n], start=(part == 0), stop=False)
                    pe.wait_ge(ut_low, m)
                    for c in range(2):
                        last = pe.matmul(ps_bu[:, c, 0:n], bt[:, 0, c, :], u_t[:, 1, 0:n], start=False, stop=True)
                    last.then_inc(bu_ready, 1)

            iters = [None]

            for q in range(U):
                step(q + 1, q)
            with pe.Fori(1, NQ // U) as i:
                first = i * U
                iters[0] = i * 32
                for q in range(U):
                    step(first + (q + 1), q)
            for m in range(NQ + 1, NQ + 6):
                step(m, (m - 1) % U)

            def split_product(out_ap, stationary, moving, start, stop, low_part, count):
                (wh, wl), (xh, xl) = stationary, moving
                pe.matmul(out_ap, wh, xh, start=start, stop=False)
                pe.matmul(out_ap, wl, xh, start=False, stop=False)
                pe.wait_ge(low_part, count)
                return pe.matmul(out_ap, wh, xl, start=False, stop=stop)

            def turn(k):
                pe.wait_ge(xn_ready, k + 1)
                wait(pe, xtl_ready, k)
                wait(pe, combined, k - 2)
                for j in range(TJ):
                    last = pe.transpose(ps_xt[:, j * 128:(j + 1) * 128], xn[:, j, :], ident)
                last.then_inc(xt_ready, 1)

            def back(k):
                pe.wait_ge(yt_copied, k + 1)
                if isinstance(k, int) and k >= NT - 2:
                    pe.wait_ge(combined, k)
                for j in range(TJ):
                    last = pe.transpose(ps_y[:, j * 128:(j + 1) * 128], y_t[:, j * 128:(j + 1) * 128], ident)
                last.then_inc(y_ready, 1)

            def first_layer(k, v, chunks):
                w = w_t[:, SLOT3[v]]
                for c in chunks:
                    wait(pe, gelu_done, k * FC + (c + 1 - FC))
                    split_product(ps_g[c], (w[:, 0, c, :], w[:, 1, c, :]), (xn_t[:, 0, :], xn_t[:, 1, :]),
                                  True, True, xtl_ready, k + 1).then_inc(up_ready, 1)

            def begin(k, v, landed):
                pe.wait_ge(w_tile_landed[v], landed)
                pe.wait_ge(xth_ready, k + 1)
                first_layer(k, v, [0])
                if not (isinstance(k, int) and k < 2):
                    back(k - 2)
                first_layer(k, v, [1])

            def tile(k, v, i=None):
                first_layer(k, v, range(2, FC))
                if not (isinstance(k, int) and k == NT - 1):
                    turn(k + 1)
                else:
                    back(k - 1)
                w = w_t[:, SLOT3[v]]
                y = ps_yt[SLOT3[v]]
                wait(pe, yt_copied, k - 1)
                for c in range(FC):
                    pe.wait_ge(high_done, k * FC + (c + 1))
                    split_product(y[:], (w[:, 2, c, :], w[:, 3, c, :]), (hidden[:, 0, c, :], hidden[:, 1, c, :]),
                                  c == 0, c == FC - 1, low_done, k * FC + (c + 1)).then_inc(down_done, 1)
                if not (isinstance(k, int) and k == NT - 1):
                    begin(k + 1, (v + 1) % V, 16 * ((k + 1) // V + 1) if i is None else
                          i * 16 + (16 if v + 1 < V else 32))

            turn(0)
            begin(0, 0, 16)
            for_tiles(pe, tile)
            back(NT - 1)

        @block.scalar
        def _(act):
            act.dma_start(vec[:], vecs).then_inc(vec_landed, 16)
            act.dma_start(pos[:], posT).then_inc(w_landed, 16)
            act.dma_start(bri[:], b_ri).then_inc(bc_landed, 16)
            act.dma_start(rhs_s[:, :, 0:HID], c_ph).then_inc(bc_landed, 16)
            act.wait_ge(memsets_done, 1)
            act.activation(warm[:], zeros[:, 0:1], ACT.Exp)
            act.wait_ge(vec_landed, 16)
            act.activation(lam[:, 0:1], vec[:, V_STEP:V_STEP + 1], ACT.Exp).then_inc(setup_act, 1)
            act.wait_ge(setup_act, 1)
            act.activation(lam[:, 1:2], vec[:, V_LR:V_LR + 1], ACT.Exp, scale=lam[:, 0:1]).then_inc(setup_act, 1)
            act.wait_ge(angles_ready, 1)
            act.activation(lam[:, 8:10], lam[:, 6:8], ACT.Sin).then_inc(setup_act, 1)
            act.wait_ge(pos_ready, 1)
            act.activation(h_t[:, HSLOT[U - 1], 0, :], zeros[:], ACT.Identity, bias=lam[:, 20:21]).then_inc(h_copied, 1)

            def high_parts(e):
                act.wait_ge(raw_landed, 32)
                wait(act, w_low, e - 1)
                src = raw[:, 0, e, :].rearrange("d (p c) -> d c p", c=FC)
                gamma = vec[:, V_GAMMA:V_GAMMA + 1]
                act.activation(w1_full[:, e % 2, :].rearrange("d (c p) -> d c p", c=FC), src, ACT.Copy, scale=gamma)
                act.activation(w_all[:, e, 0, :].rearrange("d (c p) -> d c p", c=FC), src, ACT.Copy, scale=gamma)
                act.activation(w_all[:, e, 2, :], raw[:, 1, e, :], ACT.Copy).then_inc(w_high, 1)

            def step(m, q):
                a, b, d = m - 1, m - 2, m - 4
                if exists(a):
                    act.wait_ge(norm1, m)
                    act.wait_ge(hb_ready, m)
                    wait(act, ut_ready, m - 1)
                    for t in range(steps_of(a)):
                        last = act.activation(u_b[:, t, :], ps_ht[:, t * 128:(t + 1) * 128], ACT.Identity,
                                              bias=nmr1[:, t:t + 1], scale=rs1[:, t:t + 1])
                    last.then_inc(u_ready, 1)
                if exists(m):
                    act.wait_ge(h_summed, m)
                    wait(act, v_ready, m - 1)
                    for t in range(TQ):
                        col = TQ * (m - 1) + (t + 1)
                        bias = pos[:, col:col + 1] if isinstance(m, int) else pos[:, bass.ds(col, 1)]
                        last = act.activation(h_t[:, HSLOT[q], t, :], ps_h[:, t * 128:(t + 1) * 128], ACT.Identity,
                                              bias=bias)
                    last.then_inc(h_copied, 1)
                if exists(a):
                    act.wait_ge(ut_ready, m)
                    wait(act, bu_ready, m - 1)
                    n = steps_of(a) * B
                    act.activation(u_t[:, 0, 0:n], ps_ut[:, 0:n], ACT.Copy).then_inc(ut_high, 1)
                if exists(d):
                    n = steps_of(d)
                    act.wait_ge(scaled_ready, m - 3)
                    wait(act, gate_ready, m - 4)
                    act.activation(expd[:, 0:n, :], scaled[:, 0:n, :], ACT.Exp).then_inc(exp_ready, 1)
                if exists(b):
                    act.wait_ge(out_ready, m - 1)
                    qs = slot(q, 2)
                    wait(act, rows_left, m - 7)
                    n = steps_of(b)
                    for g in range((n + 1) // 2):
                        w = min(2, n - 2 * g)
                        last = act.activation(rows[:, qs, 2 * g:2 * g + w, :],
                                              ps_o[g][:, 0:w * ROW].rearrange("p (t c) -> p t c", t=w), ACT.Copy)
                    last.then_inc(row_copied, 1)
                if isinstance(m, int) and m in (NQ + 2, NQ + 3):
                    for e in range(2) if m == NQ + 2 else range(2, E):
                        high_parts(e)

            for q in range(U):
                step(q + 1, q)
            with act.Fori(1, NQ // U) as i:
                first = i * U
                for q in range(U):
                    step(first + (q + 1), q)
            for m in range(NQ + 1, NQ + 6):
                step(m, (m - 1) % U)

            def turned_high(k):
                act.wait_ge(xt_ready, k + 1)
                wait(act, up_ready, k * FC)
                act.activation(xn_t[:, 0, :], ps_xt[:], ACT.Copy).then_inc(xth_ready, 1)

            def copy_y(k, v):
                act.wait_ge(down_done, k * FC + FC)
                wait(act, y_ready, k)
                act.activation(y_t, ps_yt[SLOT3[v]][:], ACT.Copy).then_inc(yt_copied, 1)

            def tile(k, v, i=None):
                for c in range(FC):
                    act.wait_ge(up_ready, k * FC + (c + 1))
                    wait(act, down_done, k * FC + (c + 1 - FC))
                    act.activation(hidden[:, 0, c, :], ps_g[c], ACT.Gelu).then_inc(high_done, 1)
                    act.activation(full[:, c, :], ps_g[c], ACT.Gelu).then_inc(gelu_done, 1)
                    if c == 1 and isinstance(k, int) and k == NT - 1:
                        copy_y(k - 1, (v - 1) % V)
                if not (isinstance(k, int) and k == NT - 1):
                    turned_high(k + 1)
                if not (isinstance(k, int) and k in (0, NT - 1)):
                    copy_y(k - 1, (v - 1) % V)

            act.activation(warm[:], zeros[:, 0:1], ACT.Gelu)
            turned_high(0)
            for_tiles(act, tile)
            copy_y(NT - 1, V - 1)

        @block.vector
        def _(dve):
            dve.memset(ones[:], 1.0)
            dve.memset(ones_mean[:], 1.0 / HID)
            dve.memset(eps_t[:], EPS)
            dve.memset(half_t[:], -0.5)
            dve.memset(neg_t[:], -1.0)
            dve.memset(four_t[:], float(TQ))
            dve.memset(one_e[:], 1.0)
            dve.memset(chosen[:], 0.0)
            dve.memset(filler[:], 0.0)
            dve.memset(zeros[:], 0.0).then_inc(memsets_done, 1)

            chain = [0]

            def link(ins):
                chain[0] += 1
                ins.then_inc(setup_chain, 1)
                dve.wait_ge(setup_chain, chain[0])

            def col(n):
                return lam[:, n:n + 1]

            def tt(o, x, y, op):
                return dve.tensor_tensor(o, x, y, op)

            dve.wait_ge(memsets_done, 1)
            link(dve.memset(filler[:, :, LISTED - 1:LISTED], NOWHERE))
            dve.wait_ge(setup_act, 1)
            link(tt(col(2), vec[:, V_LI:V_LI + 1], col(0), ALU.mult))
            link(dve.tensor_scalar(col(3), col(2), 0.15915494309189535, 12582912.0, ALU.mult, ALU.add))
            link(dve.tensor_scalar(col(4), col(3), -12582912.0, None, ALU.add))
            link(dve.scalar_tensor_tensor(out=col(5), in0=col(4), scalar=-6.28125, in1=col(2), op0=ALU.mult, op1=ALU.add))
            link(dve.scalar_tensor_tensor(out=col(5), in0=col(4), scalar=-0.0019353071795864769, in1=col(5),
                                          op0=ALU.mult, op1=ALU.add))
            link(dve.tensor_scalar(col(6), col(5), 3.1415925, -3.1415925, ALU.min, ALU.max))
            dve.tensor_scalar(col(7), col(6), 0.5, None, ALU.mult).then_inc(angles_ready, 1)
            lr, li = vec[:, V_LR:V_LR + 1], vec[:, V_LI:V_LI + 1]
            link(tt(col(16), lr, lr, ALU.mult))
            link(dve.scalar_tensor_tensor(out=col(16), in0=li, scalar=li, in1=col(16), op0=ALU.mult, op1=ALU.add))
            link(dve.reciprocal(col(17), col(16)))
            dve.wait_ge(w_landed, 16 * 5)
            link(tt(col(20), vec[:, V_TOK:V_TOK + 1], pos[:, 0:1], ALU.add))
            dve.tensor_scalar(pos[:, 1:SEQ], pos[:, 1:SEQ], vec[:, V_B:V_B + 1], None, ALU.add).then_inc(pos_ready, 1)
            dve.wait_ge(setup_act, 3)
            tt(col(13), col(1), col(8), ALU.mult)
            link(tt(col(10), col(9), col(9), ALU.mult))
            dve.tensor_scalar(col(14), col(13), -1.0, None, ALU.mult)
            link(dve.tensor_scalar(col(11), col(10), -2.0, 1.0, ALU.mult, ALU.add))
            link(tt(col(12), col(1), col(11), ALU.mult))
            tt(col(18), col(13), li, ALU.mult)
            link(dve.tensor_scalar(col(15), col(12), -1.0, None, ALU.add))
            tt(col(19), col(15), li, ALU.mult)
            link(dve.scalar_tensor_tensor(out=col(18), in0=col(15), scalar=lr, in1=col(18), op0=ALU.mult, op1=ALU.add))
            tt(col(18), col(18), col(17), ALU.mult)
            link(dve.scalar_tensor_tensor(out=col(19), in0=col(13), scalar=lr, in1=col(19), op0=ALU.mult,
                                          op1=ALU.subtract))
            link(tt(col(19), col(19), col(17), ALU.mult))
            dve.wait_ge(bc_landed, 32)
            dve.tensor_scalar(col(21), col(19), -1.0, None, ALU.mult)
            dve.tensor_scalar(bbar[:, 0, :], bri[:, 0, :], col(18), None, ALU.mult)
            link(dve.tensor_scalar(bbar[:, 1, :], bri[:, 1, :], col(18), None, ALU.mult))
            dve.scalar_tensor_tensor(out=bbar[:, 0, :], in0=bri[:, 1, :], scalar=col(21), in1=bbar[:, 0, :],
                                     op0=ALU.mult, op1=ALU.add)
            dve.scalar_tensor_tensor(out=bbar[:, 1, :], in0=bri[:, 0, :], scalar=col(19), in1=bbar[:, 1, :],
                                     op0=ALU.mult, op1=ALU.add)
            dve.wait_ge(setup_pe, 1)
            dve.wait_ge(consts_landed, 16)
            tt(rhs_v[:, HID:ROW], wg_sb[:], ps_rank[:, 0:E], ALU.subtract)
            dve.tensor_copy(rhs_v[:, 0:HID], ident)
            dve.tensor_copy(tri[:], cst[:, C_TRI:C_TRI + 128])
            dve.tensor_copy(base[:, 0, :], cst[:, C_BASE:C_BASE + E])
            dve.tensor_scalar(rhs_s[:, 0, 0:HID], rhs_s[:, 0, 0:HID], 2.0, None, ALU.mult)
            dve.tensor_scalar(rhs_s[:, 1, 0:HID], rhs_s[:, 1, 0:HID], -2.0, None, ALU.mult).then_inc(setup_dve, 1)
            def setup_operands():
                dve.wait_ge(setup_pe, 2)
                b_turned = ps_o[0][:, 0:256].rearrange("p (c h) -> p c h", c=2)
                link(dve.tensor_copy(bt[:, 0], b_turned))
                tt(bt[:, 1], b_turned, bt[:, 0].bitcast(F32), ALU.subtract)
                dve.wait_ge(setup_pe, 3)
                dve.tensor_scalar(rhs_s[:, 0, HID:ROW], ps_o[1][:, 0:E], 2.0, None, ALU.mult)
                dve.tensor_scalar(rhs_s[:, 1, HID:ROW], ps_o[1][:, 64:64 + E], -2.0, None, ALU.mult).then_inc(setup_dve, 1)
                dve.wait_ge(setup_dve, 2)

            re_l, im_l, neg_im_l = col(12), col(13), col(14)
            d_col = vec[:, V_D:V_D + 1]

            def bc_e(x, n):
                return x.rearrange("p (t o) -> p t o", o=1).broadcast_to([128, n, E])

            def low_parts(e):
                dve.wait_ge(w_high, e + 1)
                w = w_all[:, e]
                tt(w[:, 1, :], w1_full[:, e % 2, :], w[:, 0, :].bitcast(F32), ALU.subtract)
                tt(w[:, 3, :], raw[:, 1, e, :], w[:, 2, :].bitcast(F32), ALU.subtract).then_inc(w_low, 1)

            def plan():
                pchain = [0]

                def plink(ins):
                    pchain[0] += 1
                    ins.then_inc(plan_step, 1)
                    dve.wait_ge(plan_step, pchain[0])

                dve.wait_ge(base_ready, NQ + 1)
                cst0 = cst[0:1, :]
                plink(tt(count[:], base[0:1, 0, :], cst0[:, C_BASE:C_BASE + E], ALU.subtract))
                plink(tt(cmp_t[:], count[:].rearrange("o (e j) -> o e j", j=1).broadcast_to([1, E, MAXT]),
                         cst0[:, C_GRID:C_GRID + MAXT].rearrange("o (e j) -> o e j", e=1).broadcast_to([1, E, MAXT]),
                         ALU.is_gt))
                plink(dve.tensor_reduce(ntile[:], cmp_t[:], AX, ALU.add))
                plink(dve.tensor_tensor_scan(cum[:], one_e[:], ntile[:], 0.0, ALU.mult, ALU.add))
                grid_k = cst0[:, C_K:C_K + NT]
                plink(tt(passed[:], grid_k.rearrange("o (k e) -> o k e", e=1).broadcast_to([1, NT, E]),
                         cum[:].rearrange("o (k e) -> o k e", k=1).broadcast_to([1, NT, E]), ALU.is_ge))
                plink(dve.tensor_reduce(expert_f[:], passed[:], AX, ALU.add))
                plink(tt(before[:], passed[:], ntile[:].rearrange("o (k e) -> o k e", k=1).broadcast_to([1, NT, E]),
                         ALU.mult))
                plink(dve.tensor_reduce(before_f[:], before[:], AX, ALU.add))
                plink(tt(start_f[:, 0, :], grid_k, before_f[:], ALU.subtract))
                plink(dve.tensor_scalar(start_f[:, 1, :], expert_f[:], float(REGION), None, ALU.mult))
                plink(dve.scalar_tensor_tensor(out=start_f[:, 2, :], in0=start_f[:, 0, :], scalar=float(TILE),
                                               in1=start_f[:, 1, :], op0=ALU.mult, op1=ALU.add))
                plink(dve.tensor_scalar(start_i[:], start_f[:, 2, :], float(E * REGION), None, ALU.min))
                plink(dve.tensor_scalar(weights_f[:], expert_f[:], float(4 * FF), None, ALU.mult))
                plink(dve.tensor_scalar(weights_i[:], weights_f[:], float((E - 1) * 4 * FF), None, ALU.min))
                dve.tensor_copy(base_i[:], base[0:1, 0, :]).then_inc(plan_ready, 1)

            def step(m, q):
                a, b, c3, c4, c5 = m - 1, m - 2, m - 3, m - 4, m - 5
                if exists(a):
                    dve.wait_ge(hb_ready, m)
                    n = steps_of(a)
                    for t in range(n):
                        last = dve.bn_stats(st1[:, t, :], ps_ht[:, t * 128:(t + 1) * 128])
                    last.then_inc(stats1_parts, 1)
                if exists(c5):
                    n5 = steps_of(c5)
                    dve.wait_ge(den_ready, m - 4)
                    dve.tensor_scalar(gate_den1[:, 0:n5], gate_den[:, 0:n5], 1.0, None, ALU.add).then_inc(den1_ready, 1)
                if exists(a):
                    wait(dve, norm1, m - 1)
                    dve.wait_ge(stats1_parts, m)
                if exists(c5):
                    dve.wait_ge(den1_ready, m - 4)
                    dve.reciprocal(rows[:, slot(q, 5), 0:n5, HID + 2], gate_den1[:, 0:n5]).then_inc(gate_ready, 1)
                if exists(a):
                    for t in range(steps_of(a)):
                        last = dve.bn_aggr(mv1[:, t, :], st1[:, t, :])
                    last.then_inc(moments1, 1)
                if isinstance(m, int) and m == 1:
                    setup_operands()
                if exists(c4):
                    n4 = steps_of(c4)
                    qs4 = slot(q, 4)
                    k4 = m - 3

                    def r_scaled():
                        dve.wait_ge(rs2_ready, k4)
                        dve.wait_ge(below_ready, k4)
                        tt(scaled[:, 0:n4, :], below[:, 0:n4, :], bc_e(rs2[:, 0, 0:n4], n4), ALU.mult)\
                            .then_inc(scaled_ready, 1)

                    def r_place():
                        dve.wait_ge(rank_ready, k4)
                        wait(dve, base_ready, k4 - 1)
                        tt(place[:, 0:n4, :], ps_rank[:, 0:n4 * E].rearrange("p (t e) -> p t e", e=E),
                           base[:, 0, :].rearrange("p (o e) -> p o e", o=1).broadcast_to([128, n4, E]), ALU.add)\
                            .then_inc(place_ready, 1)

                    def r_base():
                        dve.wait_ge(place_ready, k4)
                        tt(base[:, 0, :], base[:, 0, :], ps_rank[:, TQ * E:(TQ + 1) * E], ALU.add)\
                            .then_inc(base_ready, 1)

                    def r_sum():
                        dve.wait_ge(exp_ready, k4)
                        dve.tensor_reduce(exp_sum[:, 0:n4], expd[:, 0:n4, :], AX, ALU.add).then_inc(sum_ready, 1)

                    def r_others():
                        dve.scalar_tensor_tensor(out=others[:, 0:n4, :], in0=chosen[:, 0:n4, :], scalar=0.0,
                                                 in1=expd[:, 0:n4, :], op0=ALU.is_equal, op1=ALU.mult)\
                            .then_inc(others_ready, 1)

                    def r_at():
                        tt(listed_at[:, 0:n4, :], place[:, 0:n4, :], chosen[:, 0:n4, :], ALU.mult)\
                            .then_inc(at_ready, 1)

                    def r_second():
                        dve.wait_ge(others_ready, k4)
                        dve.tensor_reduce(second[:, 0:n4], others[:, 0:n4, :], AX, ALU.max).then_inc(second_ready, 1)

                    def r_destf():
                        dve.wait_ge(at_ready, k4)
                        dve.tensor_reduce(dest_f[:, 0:n4], listed_at[:, 0:n4, :], AX, ALU.add).then_inc(destf_ready, 1)

                    def r_den():
                        dve.wait_ge(sum_ready, k4)
                        dve.wait_ge(second_ready, k4)
                        dve.scalar_tensor_tensor(out=gate_den[:, 0:n4], in0=exp_sum[:, 0:n4], scalar=GATE_EPS,
                                                 in1=second[:, 0:n4], op0=ALU.mult, op1=ALU.add).then_inc(den_ready, 1)

                    def r_dest():
                        dve.wait_ge(destf_ready, k4)
                        dve.tensor_copy(dest[:, qs4, 0:n4], dest_f[:, 0:n4]).then_inc(dest_ready, 1)

                if exists(c3):
                    n3 = steps_of(c3)
                    qs3 = slot(q, 3)
                    k3 = m - 2
                    row3 = rows[:, qs3, 0:n3, :]

                    def s_stats(ts):
                        if 0 in ts:
                            dve.wait_ge(row_copied, k3)
                        for t in ts:
                            last = dve.bn_stats(st2[:, t, :], rows[:, qs3, t, 0:HID])
                        if n3 - 1 in ts:
                            last.then_inc(stats2_parts, 1)

                    def s_top():
                        dve.tensor_reduce(top[:, 0:n3], row3[:, :, RAW:RAW + E], AX, ALU.max).then_inc(top_ready, 1)

                    def s_aggr():
                        for t in range(n3):
                            last = dve.bn_aggr(mv2[:, t, :], st2[:, t, :])
                        last.then_inc(moments2, 1)

                    def s_below():
                        wait(dve, scaled_ready, k3 - 1)
                        dve.wait_ge(stats2_parts, k3)
                        wait(dve, nmr2_ready, k3 - 1)
                        dve.wait_ge(top_ready, k3)
                        tt(below[:, 0:n3, :], row3[:, :, RAW:RAW + E], bc_e(top[:, 0:n3], n3), ALU.subtract)\
                            .then_inc(below_ready, 1)

                    def s_key():
                        dve.wait_ge(below_ready, k3)
                        dve.scalar_tensor_tensor(out=key[:, 0:n3, :], in0=below[:, 0:n3, :], scalar=0.0,
                                                 in1=tie_weight[:, 0:n3, :], op0=ALU.is_equal, op1=ALU.mult)\
                            .then_inc(key_ready, 1)

                    def s_keytop():
                        dve.wait_ge(key_ready, k3)
                        dve.tensor_reduce(key_top[:, 0:n3], key[:, 0:n3, :], AX, ALU.max).then_inc(keytop_ready, 1)

                    def s_chosen():
                        dve.wait_ge(keytop_ready, k3)
                        tt(chosen[:, 0:n3, :], key[:, 0:n3, :], bc_e(key_top[:, 0:n3], n3), ALU.is_equal)\
                            .then_inc(chosen_ready, 1)

                late = [r_place, r_base, r_at, r_destf, r_dest] if exists(c4) else []
                if exists(c3):
                    late += [lambda: s_stats(range(min(1, n3))), lambda: s_stats(range(1, min(2, n3))), s_top]

                if exists(b):
                    dve.wait_ge(bu_ready, m - 1)
                    wait(dve, out_ready, m - 2)
                    if isinstance(b, int) and b == 0:
                        dve.tensor_copy(states[:, TQ - 1, :, :], ps_bu[:, :, 0:B])
                        dve.tensor_copy(states[:, 0, :, :], ps_bu[:, :, 0:B]).then_inc(state_done, 1)
                    else:
                        for t in range(TQ):
                            T = last_t(b) - TQ + t
                            pv = (t - 1) % TQ
                            dd = decayed[:, t % 2, :, :]
                            dve.wait_ge(state_done, T)
                            dve.scalar_tensor_tensor(out=dd, in0=states[:, pv, :, :], scalar=re_l,
                                                     in1=ps_bu[:, :, t * B:(t + 1) * B], op0=ALU.mult, op1=ALU.add)\
                                .then_inc(decay_done, 1)
                            if late:
                                late.pop(0)()
                            dve.wait_ge(decay_done, T)
                            dve.scalar_tensor_tensor(out=states[:, t, 0, :], in0=states[:, pv, 1, :], scalar=neg_im_l,
                                                     in1=dd[:, 0, :], op0=ALU.mult, op1=ALU.add)
                            dve.scalar_tensor_tensor(out=states[:, t, 1, :], in0=states[:, pv, 0, :], scalar=im_l,
                                                     in1=dd[:, 1, :], op0=ALU.mult, op1=ALU.add)\
                                .then_inc(state_done, 1)
                            if late:
                                late.pop(0)()
                for f in late:
                    f()
                if exists(c3):
                    s_stats(range(2, n3))
                if exists(a):
                    dve.wait_ge(ut_high, m)
                    n = steps_of(a) * B
                    tt(u_t[:, 1, 0:n], ps_ut[:, 0:n], u_t[:, 0, 0:n].bitcast(F32), ALU.subtract).then_inc(ut_low, 1)
                if isinstance(m, int) and m == NQ + 3:
                    low_parts(0)
                    low_parts(1)
                if isinstance(m, int) and m == NQ + 4:
                    low_parts(2)
                    low_parts(3)
                    plan()
                if exists(c4):
                    r_scaled()
                if exists(c3):
                    s_below()
                    s_aggr()
                    s_key()
                if exists(c4):
                    r_sum()
                    r_others()
                if exists(c3):
                    s_keytop()
                if exists(c4):
                    r_second()
                if exists(a):
                    n = steps_of(a)
                    sv = HSLOT[slot(q, 1)]
                    wait(dve, out_ready, m - 2)
                    turned = ps_ut[:, 0:n * B].rearrange("p (t b) -> p t b", t=n)
                    dve.scalar_tensor_tensor(out=v_t[:, sv, 0:n, :], in0=turned, scalar=d_col,
                                             in1=h_t[:, sv, 0:n, :], op0=ALU.mult, op1=ALU.add).then_inc(v_ready, 1)
                if exists(c4):
                    r_den()
                if exists(c3):
                    if exists(c4):
                        dve.wait_ge(rank_ready, k4)
                    s_chosen()

            for_steps(dve, step)
            for e in range(4, E):
                low_parts(e)

            def normalise(k, v, landed, parts):
                if parts[0] == 0:
                    dve.wait_ge(tile_landed[v], landed)
                    wait(dve, xt_ready, k)
                for j in parts:
                    last = dve.tensor_scalar(xn[:, j, :], lt[:, v, j, 0:HID], lt[:, v, j, HID:HID + 1],
                                             lt[:, v, j, HID + 1:HID + 2], ALU.mult, ALU.add)
                if parts[-1] == TJ - 1:
                    last.then_inc(xn_ready, 1)

            def turned_low(k):
                dve.wait_ge(xth_ready, k + 1)
                dve.tensor_tensor(xn_t[:, 1, :], ps_xt[:], xn_t[:, 0, :].bitcast(F32), ALU.subtract)\
                    .then_inc(xtl_ready, 1)

            def combine(k, v):
                wait(dve, results_left, k - 2)
                dve.tensor_copy(place_i[:, v, :], lt[:, v, :, HID + 3]).then_inc(placei_ready, 1)
                dve.wait_ge(y_ready, k + 1)
                for j in range(TJ):
                    last = dve.scalar_tensor_tensor(out=res[:, v, j, :], in0=ps_y[:, j * 128:(j + 1) * 128],
                                                    scalar=lt[:, v, j, HID + 2:HID + 3], in1=lt[:, v, j, 0:HID],
                                                    op0=ALU.mult, op1=ALU.add)
                last.then_inc(combined, 1)

            def tile(k, v, i=None):
                if not (isinstance(k, int) and k < 2):
                    combine(k - 2, (v - 2) % V)
                nv = (v + 2) % V
                landed = 16 * ((k + 2) // V + 1) if i is None else i * 16 + (16 if v + 2 < V else 32)
                for c in range(FC):
                    dve.wait_ge(gelu_done, k * FC + (c + 1))
                    dve.tensor_tensor(hidden[:, 1, c, :], full[:, c, :], hidden[:, 0, c, :].bitcast(F32),
                                      ALU.subtract).then_inc(low_done, 1)
                    if c == 2 and isinstance(k, int) and k == NT - 1:
                        combine(k - 1, (v - 1) % V)
                    if c in NORM and not (isinstance(k, int) and k >= NT - 2):
                        normalise(k + 2, nv, landed, NORM[c])
                if not (isinstance(k, int) and k == NT - 1):
                    turned_low(k + 1)
                if not (isinstance(k, int) and k >= NT - 2):
                    normalise(k + 2, nv, landed, NORM[FC])

            NORM = {1: [0], 2: [1], FC: [2, 3]}
            normalise(0, 0, 16, range(TJ))
            turned_low(0)
            normalise(1, 1, 16, range(TJ))
            for_tiles(dve, tile)
            combine(NT - 1, V - 1)

        @block.gpsimd
        def _(pool):
            def tt(o, x, y, op):
                return pool.tensor_tensor(o, x, y, op)

            pool.wait_ge(memsets_done, 1)
            pool.wait_ge(vec_landed, 16)
            pool.tensor_copy(out_row[:, 0:1], vec[:, V_IMG:V_IMG + 1]).then_inc(outrow_ready, 1)

            def scatter(m, q, c5):
                n = steps_of(c5)
                qs = slot(q, 5)
                pool.wait_ge(gate_ready, m - 4)
                pool.wait_ge(dest_ready, m - 4)
                pool.wait_ge(meta_ready, m - 4)
                pool.sem_inc(pool_passed, 1)
                for t in range(n):
                    pool.indirect_dma_start(
                        out=lists, out_offset=bass.IndirectOffsetOnAxis(ap=dest[:, qs, t:t + 1], axis=0),
                        in_=rows[:, qs, t, 0:LISTED], in_offset=None,
                        bounds_check=E * REGION - 1, oob_is_err=True).then_inc(listed[qs], 16)

            def factors(m, q, c4):
                n = steps_of(c4)
                qs = slot(q, 4)
                k = m - 3
                pool.wait_ge(moments2, k)
                wait(pool, scaled_ready, k - 1)
                tt(ve2[:, 0, 0:n], mv2[:, 0:n, 1], eps_t[:, 0:n], ALU.add).then_inc(ve2a_ready, 1)
                tt(nm2[:, 0:n], mv2[:, 0:n, 0], neg_t[:, 0:n], ALU.mult).then_inc(nm2_ready, 1)
                pool.wait_ge(ve2a_ready, k)
                tt(ve2[:, 1, 0:n], ve2[:, 0, 0:n], eps_t[:, 0:n], ALU.mult).then_inc(ve2b_ready, 1)
                pool.wait_ge(ve2b_ready, k)
                tt(ve2[:, 1, 0:n], ve2[:, 1, 0:n], mv2[:, 0:n, 1], ALU.add).then_inc(ve2c_ready, 1)
                pool.wait_ge(ve2c_ready, k)
                tt(rs2[:, :, 0:n], ve2[:, :, 0:n], half_t[:, :, 0:n], ALU.pow).then_inc(rs2_ready, 1)
                pool.wait_ge(rs2_ready, k)
                pool.wait_ge(below_ready, k)
                pool.wait_ge(nm2_ready, k)
                tt(rows[:, qs, 0:n, HID + 1], nm2[:, 0:n], rs2[:, 1, 0:n], ALU.mult).then_inc(nmr2_ready, 1)
                pool.tensor_copy(rows[:, qs, 0:n, HID], rs2[:, 1, 0:n])
                pool.wait_ge(outrow_ready, k)
                pool.sem_inc(pool_passed, 1)
                pool.tensor_copy(rows[:, qs, 0:n, HID + 3], out_row[:, 0:n]).then_inc(meta_ready, 1)
                pool.wait_ge(meta_ready, k)
                if isinstance(m, int) and c4 == 0:
                    for t in range(TQ):
                        last = pool.tensor_scalar(out_row[:, t:t + 1], vec[:, V_IMG:V_IMG + 1], float(t + 1), None,
                                                  ALU.add)
                    last.then_inc(outrow_ready, 1)
                else:
                    tt(out_row[:], out_row[:], four_t[:], ALU.add).then_inc(outrow_ready, 1)

            def step(m, q):
                a, c4, c5 = m - 1, m - 4, m - 5
                if exists(a):
                    n = steps_of(a)
                    pool.wait_ge(moments1, m)
                    wait(pool, u_ready, m - 1)
                    tt(ve1[:, 0:n], mv1[:, 0:n, 1], eps_t[:, 0:n], ALU.add).then_inc(ve1_ready, 1)
                    tt(nm1[:, 0:n], mv1[:, 0:n, 0], neg_t[:, 0:n], ALU.mult).then_inc(nm1_ready, 1)
                    pool.wait_ge(ve1_ready, m)
                    tt(rs1[:, 0:n], ve1[:, 0:n], half_t[:, 0, 0:n], ALU.pow).then_inc(rs1_ready, 1)
                    pool.wait_ge(rs1_ready, m)
                    pool.wait_ge(nm1_ready, m)
                    tt(nmr1[:, 0:n], nm1[:, 0:n], rs1[:, 0:n], ALU.mult).then_inc(norm1, 1)
                if exists(c4):
                    factors(m, q, c4)
                j = m - 6
                if exists(j) and not (isinstance(m, int) and m > NQ + 1):
                    qs = slot(q, 6)
                    own = 16 if qs == U - 1 else 0
                    if isinstance(m, int):
                        pool.wait_ge(listed[qs], 16 * TQ * ((j - 1) // U + 1) + own)
                    else:
                        pool.wait_ge(listed[qs], iters[0] + ((16 * TQ if q == U - 1 else 0) + own))
                    pool.sem_inc(rows_left, 1)
                if exists(c5):
                    scatter(m, q, c5)

            iters = [None]
            for q in range(U):
                step(q + 1, q)
            with pool.Fori(1, NQ // U) as i:
                first = i * U
                iters[0] = i * (16 * TQ)
                for q in range(U):
                    step(first + (q + 1), q)
            for m in range(NQ + 1, NQ + 6):
                step(m, (m - 1) % U)

            def store_tile(k, v, i=0):
                pool.wait_ge(placei_ready, k + 1)
                pool.wait_ge(combined, k + 1)
                pool.sem_inc(pool_passed, 1)
                for j in range(TJ):
                    pool.indirect_dma_start(
                        out=out, out_offset=bass.IndirectOffsetOnAxis(ap=place_i[:, v, j:j + 1], axis=0),
                        in_=res[:, v, j, :], in_offset=None,
                        bounds_check=NTOK - 1, oob_is_err=False).then_inc(stored[v], 16)
                if not (isinstance(k, int) and k < 2):
                    pool.wait_ge(stored[(v - 2) % V], 16 * TJ * ((k - 2) // V + 1) if isinstance(k, int) else
                                 i * (16 * TJ) + (16 * TJ if v >= 2 else 0))
                    pool.sem_inc(results_left, 1)

            for_tiles(pool, store_tile)


def kernel(**inputs):
    import numpy as np
    import concourse.bacc as bacc
    from concourse.bass_utils import run_bass_kernel_spmd

    get = {k: np.asarray(v) for k, v in inputs.items()}
    x = get["x"].reshape(B, 3, GRID, 14, GRID, 14).transpose(2, 4, 1, 3, 5, 0).reshape(NQ, TQ, IN_DIM, B)
    x = x.transpose(0, 2, 1, 3)
    w = get["L0_tok_W"].T
    bm, cm = get["L0_attn_B"], get["L0_attn_C"]
    images = np.arange(B, dtype=np.float32) * SEQ
    consts = np.zeros((128, C_END), np.float32)
    consts[:, C_ID:C_ID + 128] = np.eye(128)
    consts[:, C_TRI:C_TRI + 128] = np.triu(np.ones((128, 128)), 1)
    consts[:, C_WT:C_WT + TQ * E] = np.tile(np.arange(E, 0, -1), TQ)
    consts[:, C_BASE:C_BASE + E] = np.arange(E) * REGION
    consts[:, C_GRID:C_GRID + MAXT] = np.arange(MAXT) * TILE
    consts[:, C_K:C_K + NT] = np.arange(NT)
    arrays = {
        "x_main": x[:, :KC * 128].reshape(NQ, KC, 128, TQ * B).transpose(0, 2, 1, 3),
        "x_tail": x[:, KC * 128:].reshape(NQ, KT, TQ * B),
        "w_main": w[:KC * 128].reshape(KC, 128, HID).transpose(1, 0, 2),
        "w_tail": w[KC * 128:],
        "vecs": np.stack([get["L0_attn_lambda_real"], get["L0_attn_lambda_imag"], get["L0_attn_log_step"][:, 0],
                          get["L0_attn_D"], get["L0_tok_b"], get["L0_tok_token"][0], get["L0_ffn_gamma"], images], 1),
        "posT": get["L0_tok_pos"].T,
        "b_ri": bm.transpose(0, 2, 1),
        "c_hp": cm.transpose(0, 2, 1),
        "c_ph": cm.transpose(1, 2, 0),
        "wg": get["L0_ffn_w_gating"],
        "w1": get["L0_ffn_w1"],
        "w2": get["L0_ffn_w2"],
        "consts": consts,
    }
    nc = bacc.Bacc("TRN2", target_bir_lowering=False, num_devices=1)
    args = []
    for name in arrays:
        a = arrays[name] = np.ascontiguousarray(arrays[name])
        args.append(nc.dram_tensor(name, a.shape, mybir.dt.from_np(a.dtype), kind="ExternalInput").ap())
    args.append(nc.dram_tensor("out", (NTOK, HID), F32, kind="ExternalOutput").ap())
    build(nc, *args)
    r = run_bass_kernel_spmd(nc, [arrays], core_ids=[0])
    return r.results[0]["out"].reshape(B, SEQ, HID)
```
